# Optimizing a Trainium2 kernel written in Bass

```python
import numpy as np
import jax
import jax.numpy as jnp

def _softmax(x, axis=-1):
    return jax.nn.softmax(x, axis=axis)

def _gelu(x):
    return jax.nn.gelu(x, approximate=True)

def _silu(x):
    return jax.nn.silu(x)

def _sigmoid(x):
    return jax.nn.sigmoid(x)

def _layernorm(x, axis=-1, eps=1e-05):
    m = jnp.mean(x, axis=axis, keepdims=True)
    v = jnp.var(x, axis=axis, keepdims=True)
    return (x - m) / jnp.sqrt(v + eps)

def _scatter_add(tgt, idx, src, axis=0):
    return tgt.at[idx].add(src)

def _segment_sum(src, seg, n):
    return jax.ops.segment_sum(src, seg, n)
kernel_name = 'mk_cond_resid_d2_seqx_r8_08b205'

def setup_inputs(seed: int=0):
    np.random.seed(seed)
    _w = jnp.asarray

    def _rec_inputs():
        import jax
        import jax.numpy as jnp
        _rk = jax.random.key(seed)
        x = -0.0003929 + 0.9999 * jax.random.normal(jax.random.fold_in(_rk, 1), (128, 32, 256), jnp.float32)
        _lenS = 32 - jax.random.randint(jax.random.fold_in(_rk, 7), (128,), 0, max(1, 32 // 4) + 1, jnp.int32)
        _lenS2 = 32 - jax.random.randint(jax.random.fold_in(_rk, 8), (128,), 0, max(1, 32 // 4) + 1, jnp.int32)
        cond_2048 = 0.00782532 + 1.00527 * jax.random.normal(jax.random.fold_in(_rk, 11), (128, 256), jnp.float32)
        return (x, cond_2048)
    x, cond_2048 = _rec_inputs()

    def _L0_cond_setup():
        import jax, jax.numpy as jnp
        import numpy as np
        HEADS = 16
        EPS = 1e-06

        def _rms_norm(x, g):
            xf = x.astype(jnp.float32)
            y = xf * jax.lax.rsqrt(jnp.mean(xf * xf, axis=-1, keepdims=True) + EPS)
            return y.astype(x.dtype) * g
        key = jax.random.key(seed)
        ks = jax.random.split(key, 6)
        b, n, dim, emb_dim = (4, 256, 256, 256)
        d_head = dim // HEADS
        return {'x': jax.random.normal(ks[0], (b, n, dim), jnp.float32), 'emb': jax.random.normal(ks[1], (b, 1, emb_dim), jnp.float32), 'W_emb': jax.random.normal(ks[2], (emb_dim, 2 * dim), jnp.float32) * emb_dim ** (-0.5), 'b_emb': jnp.zeros((2 * dim,), jnp.float32), 'g_norm': jnp.ones((dim,), jnp.float32), 'W_qkv': jax.random.normal(ks[3], (dim, 3 * dim), jnp.float32) * dim ** (-0.5), 'g_q': jnp.ones((d_head,), jnp.float32), 'g_k': jnp.ones((d_head,), jnp.float32), 'W_out': jax.random.normal(ks[4], (dim, dim), jnp.float32) * dim ** (-0.5)}
    _L0_cond_all = _L0_cond_setup()
    _L0_cond_in = {k: v for k, v in _L0_cond_all.items() if k in ('W_emb', 'b_emb', 'g_norm', 'W_qkv', 'g_q', 'g_k', 'W_out')}
    del _L0_cond_all

    def _L1_cond_setup():
        import jax, jax.numpy as jnp
        import numpy as np
        B, T, D = (16, 128, 256)
        key = jax.random.key(seed)
        k0, k1, k2, k3 = jax.random.split(key, 4)
        scale = 1.0 / np.sqrt(D)
        return {'initial_state': jax.random.normal(k0, (B, D), jnp.float32), 'inputs': jax.random.normal(k1, (B, T, D), jnp.float32), 'W_ih': jax.random.normal(k2, (D, 3 * D), jnp.float32) * scale, 'W_hh': jax.random.normal(k3, (D, 3 * D), jnp.float32) * scale, 'b_ih': jnp.zeros((3 * D,), jnp.float32), 'b_hh': jnp.zeros((3 * D,), jnp.float32)}
    _L1_cond_all = _L1_cond_setup()
    _L1_cond_in = {k: v for k, v in _L1_cond_all.items() if k in ('W_ih', 'W_hh', 'b_ih', 'b_hh')}
    del _L1_cond_all
    return {'x': x, 'cond_2048': cond_2048, 'L0_cond_W_emb': _L0_cond_in['W_emb'], 'L0_cond_b_emb': _L0_cond_in['b_emb'], 'L0_cond_g_norm': _L0_cond_in['g_norm'], 'L0_cond_W_qkv': _L0_cond_in['W_qkv'], 'L0_cond_g_q': _L0_cond_in['g_q'], 'L0_cond_g_k': _L0_cond_in['g_k'], 'L0_cond_W_out': _L0_cond_in['W_out'], 'L1_cond_W_ih': _L1_cond_in['W_ih'], 'L1_cond_W_hh': _L1_cond_in['W_hh'], 'L1_cond_b_ih': _L1_cond_in['b_ih'], 'L1_cond_b_hh': _L1_cond_in['b_hh']}

def reference(x, cond_2048, L0_cond_W_emb, L0_cond_b_emb, L0_cond_g_norm, L0_cond_W_qkv, L0_cond_g_q, L0_cond_g_k, L0_cond_W_out, L1_cond_W_ih, L1_cond_W_hh, L1_cond_b_ih, L1_cond_b_hh):
    import jax
    import jax.numpy as jnp

    def _L0_cond_ref(x, emb, W_emb, b_emb, g_norm, W_qkv, g_q, g_k, W_out):
        import jax, jax.numpy as jnp
        import numpy as np
        HEADS = 16
        EPS = 1e-06

        def _rms_norm(x, g):
            xf = x.astype(jnp.float32)
            y = xf * jax.lax.rsqrt(jnp.mean(xf * xf, axis=-1, keepdims=True) + EPS)
            return y.astype(x.dtype) * g
        b, n, dim = x.shape
        h = HEADS
        d = dim // h
        scale_shift = emb @ W_emb + b_emb
        scale, shift = jnp.split(scale_shift, 2, axis=-1)
        xn = _rms_norm(x, g_norm) * (1.0 + scale) + shift
        qkv = xn @ W_qkv
        qkv = qkv.reshape(b, n, 3, h, d)
        q, k, v = jnp.moveaxis(qkv, 2, 0)
        q = jnp.swapaxes(q, 1, 2)
        k = jnp.swapaxes(k, 1, 2)
        v = jnp.swapaxes(v, 1, 2)
        q = _rms_norm(q, g_q)
        k = _rms_norm(k, g_k)
        logits = jnp.einsum('bhqd,bhkd->bhqk', q, k) * d ** (-0.5)
        attn = jax.nn.softmax(logits, axis=-1)
        o = jnp.einsum('bhqk,bhkd->bhqd', attn, v)
        o = jnp.swapaxes(o, 1, 2).reshape(b, n, dim)
        return o + o @ W_out

    def _L1_cond_ref(initial_state, inputs, W_ih, W_hh, b_ih, b_hh):
        import jax, jax.numpy as jnp
        import numpy as np
        B, T, D = (16, 128, 256)
        "ScanOverTime(GRU cell): sequential per-timestep module call with\n            dict-state passing; merge_dict_trees stacks the per-step\n            'state_predicted' tensors along axis=1 -> [B, T, D]."

        def cell(h, x):
            gi = x @ W_ih + b_ih
            gh = h @ W_hh + b_hh
            i_r, i_z, i_n = jnp.split(gi, 3, axis=-1)
            h_r, h_z, h_n = jnp.split(gh, 3, axis=-1)
            r = jax.nn.sigmoid(i_r + h_r)
            z = jax.nn.sigmoid(i_z + h_z)
            n = jnp.tanh(i_n + r * h_n)
            h_new = (1.0 - z) * n + z * h
            return (h_new, h_new)
        xs = jnp.swapaxes(inputs, 0, 1)
        _, hs = jax.lax.scan(cell, initial_state, xs)
        return jnp.swapaxes(hs, 0, 1)
    x = x + _L0_cond_ref(x, cond_2048[:, None, :], L0_cond_W_emb, L0_cond_b_emb, L0_cond_g_norm, L0_cond_W_qkv, L0_cond_g_q, L0_cond_g_k, L0_cond_W_out)
    x = x + _L1_cond_ref(cond_2048, x, L1_cond_W_ih, L1_cond_W_hh, L1_cond_b_ih, L1_cond_b_hh)
    return x

_drawn_inputs = setup_inputs


def setup_inputs(seed=0):
    import zlib

    import numpy as np

    out = dict(_drawn_inputs(seed))
    spreads = {'L0_cond_b_emb': (0.0, 0.1),
     'L0_cond_g_norm': (1.0, 0.2),
     'L0_cond_g_q': (1.0, 0.2),
     'L0_cond_g_k': (1.0, 0.2),
     'L1_cond_b_ih': (0.0, 0.318),
     'L1_cond_b_hh': (0.0, 0.46)}
    factors = {}
    for name, (base, spread) in spreads.items():
        noise = np.random.default_rng([zlib.crc32(name.encode()), seed]).standard_normal(out[name].shape)
        drawn = base * np.exp(spread * noise) if base else spread * noise
        out[name] = jnp.asarray(drawn.astype(out[name].dtype))
    for name, factor in factors.items():
        out[name] = (out[name] * factor).astype(out[name].dtype)
    return out
```

```python
from contextlib import ExitStack

import concourse.bass as bass
from concourse import mybir

F32 = mybir.dt.float32
F32R = mybir.dt.float32r
ALU = mybir.AluOpType
ACT = mybir.ActivationFunctionType
AX_X = mybir.AxisListType.X

P = 128
B, T, D = 128, 32, 256
HEADS, DH = 16, 16
KC = D // P
GB = P // T
NG = B // GB
HC = HEADS // KC
BANK = 512
VW = DH + 1
RMS_EPS = 1e-6

LAG_X, LAG_MOD, LAG_QKV, LAG_S, LAG_PV, LAG_OUT = 0, 1, 2, 4, 5, 6
UNROLL = 4
FIRST_LOOPED = 8


def adaptive_attention_gru(
    nc: bass.Bass, x, cond, w_emb, b_emb, g_norm, w_qkv, g_q, g_k, w_out, w_ih, w_hh, b_ih, b_hh, out,
):
    ctx = ExitStack()
    with ctx:
        def sb(name, shape, dt=F32):
            return ctx.enter_context(nc.sbuf_tensor(name, shape, dt))

        def bank(name):
            return ctx.enter_context(nc.psum_tensor(name, [P, BANK], F32))

        def sem(name):
            return ctx.enter_context(nc.semaphore(name))

        ident = sb("ident", [P, P])
        stage_w = sb("stage_w", [P, KC, 3 * D])
        stage_wo = sb("stage_wo", [P, KC, D])
        w_emb_sb = sb("w_emb_sb", [P, KC, 2 * D])
        w_hh_sb = sb("w_hh_sb", [P, KC, 3 * D])
        wqkv_hi = sb("wqkv_hi", [P, KC, 3 * D], F32R)
        wqkv_lo = sb("wqkv_lo", [P, KC, 3 * D], F32R)
        wo_hi = sb("wo_hi", [P, KC, D], F32R)
        wo_lo = sb("wo_lo", [P, KC, D], F32R)
        wih_hi = sb("wih_hi", [P, KC, 3 * D], F32R)
        wih_lo = sb("wih_lo", [P, KC, 3 * D], F32R)
        cond_sb = sb("cond_sb", [P, D])
        vec_rows = sb("vec_rows", [20, P])
        vec_cols = sb("vec_cols", [P, 20])
        bih, bhh = vec_cols[:, 0:6], vec_cols[:, 6:12]
        bemb = vec_cols[:, 12:16]
        gnorm = vec_cols[:, 16:18]
        gq_col, gk_col = vec_cols[:, 18:19], vec_cols[:, 19:20]
        bemb1 = sb("bemb1", [P, KC])
        gqk = sb("gqk", [P, 1])
        bsum = sb("bsum", [P, 4])
        bneg = sb("bneg", [P, 4])
        mod_scale = sb("mod_scale", [P, KC, NG, GB])
        mod_shift = sb("mod_shift", [P, KC, NG, GB])
        h = sb("h", [P, 2, KC, B])

        x_in = sb("x_in", [P, NG, D])
        square_x = sb("square_x", [P, D])
        xhat = sb("xhat", [P, 2, D])
        xmod = sb("xmod", [P, 2, D])
        xn = sb("xn", [P, 2, D])
        xn_hi = sb("xn_hi", [P, 2, D], F32R)
        xn_lo = sb("xn_lo", [P, 2, D], F32R)
        NS = 2 * HEADS + 1
        square_qk = sb("square_qk", [P, 2 * D])
        ss = sb("ss", [P, 2, NS])
        ms = sb("ms", [P, 2, NS])
        ln_ms = sb("ln_ms", [P, 2, NS])
        rs0 = sb("rs0", [P, 2, NS])
        newton_a = sb("newton_a", [P, 2, NS])
        newton_b = sb("newton_b", [P, 2, NS])
        rs = sb("rs", [P, 2, NS])
        qkn = sb("qkn", [P, 2, 2 * D])
        kT = sb("kT", [P, 2, D])
        qT = sb("qT", [P, 4, D])
        k_diag = sb("k_diag", [P, 2, KC * GB, HC, T])
        v_diag = sb("v_diag", [P, 4, GB, HEADS, VW])
        row_max = sb("row_max", [P, 2, HEADS])
        logits = sb("logits", [P, 2, HEADS * T])
        probs = sb("probs", [P, 2, HEADS * T])
        probsT = sb("probsT", [P, 2, HEADS, T])
        inv_sum = sb("inv_sum", [P, 2, HEADS])
        o_sb = sb("o_sb", [P, 2, D])
        oT = sb("oT", [P, 2, D])
        oT_hi = sb("oT_hi", [P, 2, D], F32R)
        oT_lo = sb("oT_lo", [P, 2, D], F32R)
        x2 = sb("x2", [P, 2, D])
        x2T = sb("x2T", [P, KC * T * B])

        pair_hi = sb("pair_hi", [P, 2, KC, 2 * B], F32R)
        pair_lo = sb("pair_lo", [P, 2, KC, 2 * B], F32R)
        freed = k_diag[:, :, :, :, :].rearrange("p s j h k -> p (s j h k)")
        taken = [0]

        def gru_tile(*shape):
            n = 1
            for size in shape:
                n *= size
            flat = freed[:, taken[0]:taken[0] + n]
            taken[0] += n
            names = " ".join("abc"[:len(shape)])
            sizes = {k: v for k, v in zip("abc", shape)}
            return flat.rearrange(f"p ({names}) -> p {names}", **sizes)

        r_g, z_g, omz, rh, npre, n_g, zh, zn = (gru_tile(KC, B) for _ in range(8))
        yT = gru_tile(2, KC, B)
        y_out = gru_tile(2, 2, D)

        banks = [bank(f"bank{i}") for i in range(8)]
        p_xT, p_qk, p_v, p_qkT, p_s, p_o, p_w, p_x2T = banks

        x_loaded = [sem(f"x_loaded{i}") for i in range(8)]
        cond_loaded = sem("cond_loaded")
        emb_loaded = sem("emb_loaded")
        vec_loaded = sem("vec_loaded")
        qkv_loaded = sem("qkv_loaded")
        wo_loaded = sem("wo_loaded")
        ih_loaded = sem("ih_loaded")
        hh_loaded = sem("hh_loaded")
        ident_zero = sem("ident_zero")
        ident_ready = sem("ident_ready")
        condT_ps = sem("condT_ps")
        condT_ready = sem("condT_ready")
        emb_ps = sem("emb_ps")
        vec_ps = sem("vec_ps")
        vec_cols_ready = sem("vec_cols_ready")
        vec_ready = sem("vec_ready")
        mod_ready = sem("mod_ready")
        diag_clear = sem("diag_clear")
        ones_ready = sem("ones_ready")
        wqkv_hi_ready = sem("wqkv_hi_ready")
        wqkv_ready = sem("wqkv_ready")
        wo_sum = sem("wo_sum")
        wo_hi_ready = sem("wo_hi_ready")
        wo_ready = sem("wo_ready")
        wih_hi_ready = sem("wih_hi_ready")
        wih_ready = sem("wih_ready")
        gru_bias = sem("gru_bias")
        gru_bias_ready = sem("gru_bias_ready")

        ssx_ready = sem("ssx_ready")
        ssqk_ready = sem("ssqk_ready")
        ms_ready = sem("ms_ready")
        ln_ready = sem("ln_ready")
        rs0_ready = sem("rs0_ready")
        newton_step = sem("newton_step")
        rs_ready = sem("rs_ready")
        xhat_ready = sem("xhat_ready")
        xT_ps = sem("xT_ps")
        xmod_ready = sem("xmod_ready")
        xn_ready = sem("xn_ready")
        xn_hi_ready = sem("xn_hi_ready")
        xn_lo_ready = sem("xn_lo_ready")
        qk_ps = sem("qk_ps")
        v_ps = sem("v_ps")
        sq_ready = sem("sq_ready")
        qkn_ready = sem("qkn_ready")
        v_ready = sem("v_ready")
        qkT_ps = sem("qkT_ps")
        kT_ready = sem("kT_ready")
        qT_ready = sem("qT_ready")
        k_diag_ready = [sem("k_diag_ready0"), sem("k_diag_ready1")]
        s_ps = sem("s_ps")
        max_ready = sem("max_ready")
        logits_ready = sem("logits_ready")
        probs_ready = sem("probs_ready")
        probsT_ready = sem("probsT_ready")
        o_ps = sem("o_ps")
        inv_ready = sem("inv_ready")
        o_ready = sem("o_ready")
        oT_ready = sem("oT_ready")
        oT_hi_ready = sem("oT_hi_ready")
        oT_lo_ready = sem("oT_lo_ready")
        w_ps = sem("w_ps")
        x2_ready = sem("x2_ready")
        x2T_ps = sem("x2T_ps")
        x2T_ready = sem("x2T_ready")

        gates_ps = [sem(f"gates_ps{c}") for c in range(KC)]
        r_ready = [sem(f"r_ready{c}") for c in range(KC)]
        z_ready = [sem(f"z_ready{c}") for c in range(KC)]
        omz_ready = [sem(f"omz_ready{c}") for c in range(KC)]
        rh_ready = [sem(f"rh_ready{c}") for c in range(KC)]
        npre_ready = [sem(f"npre_ready{c}") for c in range(KC)]
        n_ready = [sem(f"n_ready{c}") for c in range(KC)]
        zh_ready = [sem(f"zh_ready{c}") for c in range(KC)]
        zn_ready = [sem(f"zn_ready{c}") for c in range(KC)]
        h_ready = [sem(f"h_ready{c}") for c in range(KC)]
        pair_hi_ready = sem("pair_hi_ready")
        pair_lo_ready = sem("pair_lo_ready")
        yT_ready = sem("yT_ready")
        y_ps = sem("y_ps")
        y_ready = sem("y_ready")
        out_done = [sem("out_done0"), sem("out_done1")]

        def group(base, u, lag, count=NG):
            g = base + (u - lag)
            if isinstance(g, int) and not 0 <= g < count:
                return None
            return g

        def later(g, n):
            return not isinstance(g, int) or g >= n

        def spread(g, slot):
            return (g - slot) * (8 * HC) + 16 * HC

        def pipeline(eng, body, last):
            for i in range(FIRST_LOOPED):
                body(i - i % UNROLL, i % UNROLL)
            with eng.Fori(FIRST_LOOPED // UNROLL, NG // UNROLL) as q:
                for u in range(UNROLL):
                    body(q * UNROLL, u)
            for i in range(NG, last + 1):
                body(i - i % UNROLL, i % UNROLL)

        def norm_columns(n):
            if isinstance(n, int):
                return (0 if n >= LAG_QKV else NS - 1), (NS if n < NG else NS - 1)
            return 0, NS

        def gru_bank(pair_slot, chunk, part):
            return banks[4 * pair_slot + 2 * chunk + part]

        def pair_index(base, n):
            return (base // 4) * 2 + n if isinstance(base, int) else turn[0] * 2 + n

        def has_pair(base, n):
            return not isinstance(base, int) or base // 2 + n < T // 2

        def x2T_pair(u):
            return x2T[:, :].rearrange("p (c u n) -> p c u n", c=KC, n=2 * B)[:, :, u, :]

        turn = [0]

        def gru_steps(eng, body):
            for s in range(4):
                body(0, s)
            with eng.Fori(1, T // 4 - 1) as q:
                turn[0] = q
                for s in range(4):
                    body(q * 4, s)
            for s in range(4):
                body(T - 4, s)

        R_COL, Z_COL, IN_COL, HN_COL, SPARE_COL = 0, 2 * B, 0, 2 * B, 3 * B

        block = ctx.enter_context(nc.Block())

        @block.sync
        def _(sp):
            x_groups = x.rearrange("(g b) t d -> (b t) g d", b=GB)

            def load_x(i):
                n = NG // len(x_loaded)
                sp.dma_start(x_in[:, n * i:n * i + n, :], x_groups[:, n * i:n * i + n, :]).then_inc(x_loaded[i], 16)

            sp.dma_start(cond_sb[:, :], cond).then_inc(cond_loaded, 16)
            load_x(0)
            sp.dma_start(stage_w[:, :, :], w_qkv.rearrange("(c p) n -> p c n", p=P)).then_inc(qkv_loaded, 16)
            load_x(1)
            sp.dma_start(stage_wo[:, :, :], w_out.rearrange("(c p) n -> p c n", p=P)).then_inc(wo_loaded, 16)
            load_x(2)
            sp.dma_start(w_hh_sb[:, :, :], w_hh.rearrange("(c p) n -> p c n", p=P)).then_inc(hh_loaded, 16)
            for i in range(3, len(x_loaded)):
                load_x(i)
            sp.wait_ge(wqkv_ready, 1)
            sp.dma_start(stage_w[:, :, :], w_ih.rearrange("(c p) n -> p c n", p=P)).then_inc(ih_loaded, 16)

            sp.wait_ge(ones_ready, 1)

            def body(base, u):
                g = group(base, u, LAG_QKV)
                if g is not None:
                    slot = (u - LAG_QKV) % 2
                    sp.wait_ge(kT_ready, g + 1)
                    for hd in range(HC):
                        rows = slice(DH * hd, DH * hd + DH)
                        sp.dma_start(k_diag[rows, slot, :, hd, :],
                                     kT[rows, slot, :].rearrange("p (j k) -> p j k", k=T)).then_inc(k_diag_ready[slot], 16)

            pipeline(sp, body, NG - 1 + LAG_QKV)

            with sp.Fori(0, T // 4) as q:
                for slot in range(2):
                    sp.wait_ge(y_ready, q * 4 + 2 * slot + 2)
                    sp.wait_ge(x2T_ready, NG)
                    sp.dma_start(out[:, :, :].rearrange("b (u e) d -> b u (e d)", e=2)[:, q * 2 + slot, :],
                                 y_out[:, slot, :, :].rearrange("p e d -> p (e d)")).then_inc(out_done[slot], 16)
            for slot in range(2):
                sp.wait_ge(out_done[slot], 16 * (T // 4))

        @block.gpsimd
        def _(pool):
            pool.memset(ident[:, :], 0.0).then_inc(ident_zero, 1)
            pool.wait_ge(ident_zero, 1)
            pool.affine_select(out=ident[:, :], in_=ident[:, :], compare_op=ALU.not_equal, fill=1.0, base=0,
                               pattern=[[-1, P]], channel_multiplier=1).then_inc(ident_ready, 1)

            def split_late_weights():
                pool.wait_ge(ih_loaded, 16)
                pool.tensor_copy(wih_hi[:, :, :], stage_w[:, :, :]).then_inc(wih_hi_ready, 1)
                pool.wait_ge(wih_hi_ready, 1)
                pool.tensor_tensor(wih_lo[:, :, :], stage_w[:, :, :], wih_hi[:, :, :].bitcast(F32),
                                   ALU.subtract).then_inc(wih_ready, 1)

            def body(base, u):
                g = group(base, u, LAG_MOD)
                if g is not None:
                    slot = (u - LAG_MOD) % 2
                    shift = mod_shift[:, :, g, :].unsqueeze(3).broadcast_to([P, KC, GB, T])
                    pool.wait_ge(xmod_ready, g + 1)
                    if later(g, 2):
                        pool.wait_ge(xn_lo_ready, g - 1)
                    pool.tensor_tensor(xn[:, slot, :].rearrange("p (c b t) -> p c b t", c=KC, b=GB),
                                       xmod[:, slot, :].rearrange("p (c b t) -> p c b t", c=KC, b=GB),
                                       shift, ALU.add).then_inc(xn_ready, 1)
                    pool.wait_ge(xn_hi_ready, g + 1)
                    if later(g, 2):
                        pool.wait_ge(v_ps, g - 1)
                    pool.tensor_tensor(xn_lo[:, slot, :], xn[:, slot, :], xn_hi[:, slot, :].bitcast(F32),
                                       ALU.subtract).then_inc(xn_lo_ready, 1)
                g = group(base, u, LAG_PV)
                if g is not None:
                    slot = (u - LAG_PV) % 2
                    pool.wait_ge(oT_hi_ready, g + 1)
                    if later(g, 2):
                        pool.wait_ge(w_ps, g - 1)
                    pool.tensor_tensor(oT_lo[:, slot, :].rearrange("p (c b t) -> p b c t", c=KC, b=GB),
                                       oT[:, slot, :].rearrange("p (b c t) -> p b c t", c=KC, b=GB),
                                       oT_hi[:, slot, :].bitcast(F32).rearrange("p (c b t) -> p b c t", c=KC, b=GB),
                                       ALU.subtract).then_inc(oT_lo_ready, 1)
                if isinstance(base, int) and base + u == LAG_QKV:
                    split_late_weights()

            pool.wait_ge(mod_ready, 1)
            pipeline(pool, body, NG - 1 + LAG_PV)
            pool.wait_ge(x2T_ready, NG)

            def split_pair(u, slot):
                pool.wait_ge(pair_hi_ready, u + 1)
                pool.tensor_tensor(pair_lo[:, slot, :, :], x2T_pair(u), pair_hi[:, slot, :, :].bitcast(F32),
                                   ALU.subtract).then_inc(pair_lo_ready, 1)

            split_pair(0, 0)
            split_pair(1, 1)

            def step(base, s):
                t = base + s
                for c in range(KC):
                    pool.wait_ge(z_ready[c], t + 1)
                    pool.tensor_tensor(zh[:, c, :], z_g[:, c, :], h[:, (s + 1) % 2, c, :],
                                       ALU.mult).then_inc(zh_ready[c], 1)
                if s % 2 == 1 and has_pair(base, s // 2 + 2):
                    split_pair(pair_index(base, s // 2 + 2), s // 2)
                pool.wait_ge(h_ready[0], t + 1)
                pool.wait_ge(h_ready[1], t + 1)
                if later(t, 2):
                    pool.wait_ge(y_ps, t - 1)
                pool.tensor_tensor(yT[:, s % 2, :, :], h[:, s % 2, :, :],
                                   x2T[:, :].rearrange("p (c t b) -> p c t b", c=KC, b=B)[:, :, t, :],
                                   ALU.add).then_inc(yT_ready, 1)

            gru_steps(pool, step)

        @block.scalar
        def _(act):
            act.dma_start(w_emb_sb[:, :, :], w_emb.rearrange("(c p) n -> p c n", p=P)).then_inc(emb_loaded, 16)
            for row, vector in ((0, b_ih), (6, b_hh), (12, b_emb), (16, g_norm)):
                n = vector.shape[0] // P
                act.dma_start(vec_rows[row:row + n, :], vector.rearrange("(n p) -> n p", p=P)).then_inc(vec_loaded, 16)
            for row, gain in ((18, g_q), (19, g_k)):
                act.dma_start(vec_rows[row:row + 1, :].rearrange("o (h d) -> o h d", d=DH),
                              gain.unsqueeze(0).unsqueeze(0).broadcast_to([1, HC, DH])).then_inc(vec_loaded, 16)
            act.preload_act_table_set("natural_log_exp_and_others")
            act.wait_ge(vec_ps, 1)
            act.copy(vec_cols[:, :], p_o[:, 0:20]).then_inc(vec_cols_ready, 1)
            act.wait_ge(condT_ps, 1)
            act.copy(h[:, 1, :, :], p_w[:, 0:KC * B].rearrange("p (c b) -> p c b", c=KC)).then_inc(condT_ready, 1)
            act.wait_ge(qkv_loaded, 16)
            act.copy(wqkv_hi[:, :, :], stage_w[:, :, :]).then_inc(wqkv_hi_ready, 1)

            def body(base, u):
                n = group(base, u, LAG_X)
                nslot = u % 2
                if n is not None:
                    if isinstance(n, int):
                        if n % 4 == 0:
                            act.wait_ge(x_loaded[n // 4], 16)
                        if n == FIRST_LOOPED - 1:
                            for loaded in x_loaded[2:]:
                                act.wait_ge(loaded, 16)
                    if later(n, 2):
                        act.wait_ge(ms_ready, n - 1)
                    if later(n, 1):
                        act.wait_ge(ssx_ready, n)
                g = group(base, u, LAG_PV)
                if g is not None:
                    slot = (u - LAG_PV) % 2
                    act.wait_ge(logits_ready, g + 1)
                    if later(g, 2):
                        act.wait_ge(probsT_ready, g - 1)
                    act.activation(probs[:, slot, :], logits[:, slot, :], ACT.Exp).then_inc(probs_ready, 1)
                if n is not None:
                    act.activation(square_x[:, :], x_in[:, n, :], ACT.Square, scale=(DH / D) ** 0.5,
                                   accum_out=ss[:, nslot, NS - 1:NS]).then_inc(ssx_ready, 1)
                g = group(base, u, LAG_QKV)
                if g is not None:
                    act.wait_ge(qk_ps, g + 1)
                    if later(g, 1):
                        act.wait_ge(ssqk_ready, g)
                    act.activation(square_qk[:, :], p_qk[:, :], ACT.Square).then_inc(sq_ready, 1)

                def values(sequences):
                    for b in sequences:
                        rows = slice(T * b, T * b + T)
                        last = act.copy(v_diag[rows, (u - LAG_QKV) % 4, b, :, 0:DH],
                                        p_v[rows, 0:D].rearrange("p (h d) -> p h d", h=HEADS))
                    return last

                if g is not None:
                    act.wait_ge(v_ps, g + 1)
                    if later(g, 4):
                        act.wait_ge(o_ps, g - 3)
                    if isinstance(g, int) and g == 0:
                        act.wait_ge(ones_ready, 2)
                    values(range(0, 2))
                n = group(base, u, LAG_X, NG + LAG_QKV)
                if n is not None:
                    lo, hi = norm_columns(n)
                    act.wait_ge(ms_ready, n + 1)
                    act.activation(ln_ms[:, nslot, lo:hi], ms[:, nslot, lo:hi], ACT.Ln).then_inc(ln_ready, 1)
                    act.wait_ge(ln_ready, n + 1)
                    if later(n, 2):
                        act.wait_ge(rs_ready, n - 1)
                    act.activation(rs0[:, nslot, lo:hi], ln_ms[:, nslot, lo:hi], ACT.Exp,
                                   scale=-0.5).then_inc(rs0_ready, 1)
                if g is not None:
                    values(range(2, GB)).then_inc(v_ready, 1)
                n = group(base, u, LAG_X)
                if n is not None:
                    act.wait_ge(rs_ready, n + 1)
                    if later(n, 2):
                        act.wait_ge(xT_ps, n - 1)
                g = group(base, u, LAG_MOD)
                if g is not None:
                    slot = (u - LAG_MOD) % 2
                    if later(g, 2):
                        act.wait_ge(v_ps, g - 1)
                    act.wait_ge(xn_ready, g + 1)
                    act.copy(xn_hi[:, slot, :], xn[:, slot, :]).then_inc(xn_hi_ready, 1)
                if n is not None:
                    act.activation(xhat[:, nslot, :], x_in[:, n, :], ACT.Copy,
                                   scale=rs[:, nslot, NS - 1:NS]).then_inc(xhat_ready, 1)
                g = group(base, u, LAG_QKV)
                if g is not None:
                    slot = (u - LAG_QKV) % 2
                    act.wait_ge(qkT_ps, g + 1)
                    if later(g, 2):
                        act.wait_ge(k_diag_ready[slot], spread(g - 2, slot))
                    act.copy(kT[:, (u - LAG_QKV) % 2, :], p_qkT[:, D:2 * D]).then_inc(kT_ready, 1)
                    if later(g, 4):
                        act.wait_ge(s_ps, g - 3)
                d = group(base, u, LAG_OUT)
                if d is not None:
                    act.wait_ge(x2T_ps, d + 1)
                if g is not None:
                    act.activation(qT[:, (u - LAG_QKV) % 4, :], p_qkT[:, 0:D], ACT.Copy,
                                   scale=gqk[:, 0:1]).then_inc(qT_ready, 1)
                if d is not None:
                    act.copy(x2T[:, :].rearrange("p (c t g b) -> p c t g b", c=KC, t=T, b=GB)[:, :, :, d, :],
                             p_x2T[:, 0:D].rearrange("p (c b t) -> p c t b", c=KC, b=GB)).then_inc(x2T_ready, 1)
                g = group(base, u, LAG_PV)
                if g is not None:
                    slot = (u - LAG_PV) % 2
                    act.wait_ge(oT_ready, g + 1)
                    if later(g, 2):
                        act.wait_ge(w_ps, g - 1)
                    act.copy(oT_hi[:, slot, :].rearrange("p (c b t) -> p b c t", c=KC, b=GB),
                             oT[:, slot, :].rearrange("p (b c t) -> p b c t", c=KC, b=GB))\
                       .then_inc(oT_hi_ready, 1)

            act.wait_ge(vec_ready, 1)
            pipeline(act, body, NG - 1 + LAG_OUT)

            act.preload_act_table(ACT.Sigmoid)
            act.wait_ge(gru_bias_ready, 1)
            act.wait_ge(x2T_ready, NG)

            def split_pair(u, slot):
                act.copy(pair_hi[:, slot, :, :], x2T_pair(u)).then_inc(pair_hi_ready, 1)

            split_pair(0, 0)
            split_pair(1, 1)

            def step(base, s):
                t = base + s
                pair_slot, e = s // 2, s % 2
                for c in range(KC):
                    rz, xnh = gru_bank(pair_slot, c, 0), gru_bank(pair_slot, c, 1)
                    r_in = rz[:, R_COL + e * B:R_COL + e * B + B]
                    z_in = rz[:, Z_COL + e * B:Z_COL + e * B + B]
                    act.wait_ge(gates_ps[c], t + 1)
                    act.activation(r_g[:, c, :], r_in, ACT.Sigmoid, bias=bsum[:, c:c + 1]).then_inc(r_ready[c], 1)
                    act.activation(z_g[:, c, :], z_in, ACT.Sigmoid,
                                   bias=bsum[:, KC + c:KC + c + 1]).then_inc(z_ready[c], 1)
                    act.activation(omz[:, c, :], z_in, ACT.Sigmoid, bias=bneg[:, KC + c:KC + c + 1],
                                   scale=-1.0).then_inc(omz_ready[c], 1)
                    act.wait_ge(npre_ready[c], t + 1)
                    act.activation(n_g[:, c, :], npre[:, c, :], ACT.Tanh,
                                   bias=bih[:, 2 * KC + c:2 * KC + c + 1]).then_inc(n_ready[c], 1)
                    if c == 0 and s % 2 == 1 and has_pair(base, s // 2 + 2):
                        split_pair(pair_index(base, s // 2 + 2), s // 2)
                if later(t, 1):
                    store_step(t - 1, (s - 1) % 4, 1 - pair_slot)

            def store_step(t, s, pair_slot):
                act.wait_ge(y_ps, t + 1)
                if s % 2 == 0 and later(t, 4):
                    act.wait_ge(out_done[s // 2], (t - s) * 4)
                for c in range(KC):
                    last = act.copy(y_out[:, s // 2, s % 2, c * P:c * P + P],
                                    gru_bank(pair_slot, c, 1)[:, SPARE_COL:SPARE_COL + P])
                last.then_inc(y_ready, 1)

            gru_steps(act, step)
            store_step(T - 1, 3, 0)

        @block.vector
        def _(dve):
            dve.memset(k_diag[:, :, :, :, :], 0.0).then_inc(ones_ready, 1)
            dve.memset(v_diag[:, :, :, :, :], 0.0).then_inc(diag_clear, 1)
            dve.wait_ge(diag_clear, 1)
            for b in range(GB):
                last = dve.memset(v_diag[T * b:T * b + T, :, b, :, DH:VW], 1.0)
            last.then_inc(ones_ready, 1)
            dve.wait_ge(vec_cols_ready, 1)
            dve.scalar_tensor_tensor(out=gqk[:, :], in0=gq_col, scalar=DH ** -0.5, in1=gk_col,
                                     op0=ALU.mult, op1=ALU.mult).then_inc(vec_ready, 1)
            dve.tensor_scalar(bemb1[:, :], bemb[:, 0:KC], 1.0, None, ALU.add).then_inc(vec_ready, 1)
            dve.wait_ge(emb_ps, 1)
            dve.wait_ge(vec_ready, 2)
            for c in range(KC):
                dve.tensor_scalar(mod_scale[:, c, :, :].rearrange("p g b -> p (g b)"), p_s[:, c * B:c * B + B],
                                  bemb1[:, c:c + 1], gnorm[:, c:c + 1], ALU.add, ALU.mult)
            for c in range(KC):
                last = dve.tensor_scalar(mod_shift[:, c, :, :].rearrange("p g b -> p (g b)"),
                                         p_s[:, (KC + c) * B:(KC + c) * B + B], bemb[:, KC + c:KC + c + 1], None,
                                         ALU.add)
            last.then_inc(mod_ready, 1)
            dve.wait_ge(mod_ready, 1)
            dve.wait_ge(wqkv_hi_ready, 1)
            dve.tensor_tensor(wqkv_lo[:, :, :], stage_w[:, :, :], wqkv_hi[:, :, :].bitcast(F32),
                              ALU.subtract).then_inc(wqkv_ready, 1)

            def output_weights():
                dve.wait_ge(wo_loaded, 16)
                dve.wait_ge(ident_ready, 1)
                for c in range(KC):
                    last = dve.tensor_tensor(stage_wo[:, c, c * P:c * P + P], stage_wo[:, c, c * P:c * P + P],
                                             ident[:, :], ALU.add)
                last.then_inc(wo_sum, 1)
                dve.wait_ge(wo_sum, 1)
                dve.tensor_copy(wo_hi[:, :, :], stage_wo[:, :, :]).then_inc(wo_hi_ready, 1)
                dve.wait_ge(wo_hi_ready, 1)
                dve.tensor_tensor(wo_lo[:, :, :], stage_wo[:, :, :], wo_hi[:, :, :].bitcast(F32),
                                  ALU.subtract).then_inc(wo_ready, 1)

            def gru_biases():
                dve.tensor_tensor(bsum[:, :], bih[:, 0:2 * KC], bhh[:, 0:2 * KC], ALU.add).then_inc(gru_bias, 1)
                dve.wait_ge(gru_bias, 1)
                dve.tensor_scalar(bneg[:, :], bsum[:, :], -1.0, None, ALU.mult).then_inc(gru_bias_ready, 1)

            def body(base, u):
                g = group(base, u, LAG_PV)
                if g is not None:
                    slot = (u - LAG_PV) % 2
                    s_heads = p_s[:, :].rearrange("p (h k) -> p h k", h=HEADS)
                    dve.wait_ge(s_ps, g + 1)
                    dve.tensor_reduce(row_max[:, slot, :], s_heads, AX_X, ALU.max).then_inc(max_ready, 1)
                    dve.wait_ge(max_ready, g + 1)
                    if later(g, 2):
                        dve.wait_ge(probs_ready, g - 1)
                    dve.tensor_tensor(logits[:, slot, :].rearrange("p (h k) -> p h k", h=HEADS), s_heads,
                                      row_max[:, slot, :].unsqueeze(2).broadcast_to([P, HEADS, T]),
                                      ALU.subtract).then_inc(logits_ready, 1)
                    dve.wait_ge(probs_ready, g + 1)
                    if later(g, 2):
                        dve.wait_ge(o_ps, g - 1)
                    dve.transpose(probsT[:, slot, :, :].rearrange("p h q -> p (h q)"), probs[:, slot, :])\
                       .then_inc(probsT_ready, 1)
                g = group(base, u, LAG_MOD)
                if g is not None:
                    slot = (u - LAG_MOD) % 2
                    dve.wait_ge(xT_ps, g + 1)
                    if later(g, 2):
                        dve.wait_ge(xn_ready, g - 1)
                    dve.tensor_tensor(xmod[:, slot, :].rearrange("p (c b t) -> p c b t", c=KC, b=GB),
                                      p_xT[:, 0:D].rearrange("p (c b t) -> p c b t", c=KC, b=GB),
                                      mod_scale[:, :, g, :].unsqueeze(3).broadcast_to([P, KC, GB, T]),
                                      ALU.mult).then_inc(xmod_ready, 1)
                g = group(base, u, LAG_QKV)
                nslot = u % 2
                if g is not None:
                    dve.wait_ge(sq_ready, g + 1)
                    dve.tensor_reduce(ss[:, nslot, 0:2 * HEADS],
                                      square_qk[:, :].rearrange("p (h d) -> p h d", d=DH),
                                      AX_X, ALU.add).then_inc(ssqk_ready, 1)
                n = group(base, u, LAG_X, NG + LAG_QKV)
                if n is not None:
                    lo, hi = norm_columns(n)
                    if g is not None:
                        dve.wait_ge(ssqk_ready, g + 1)
                    if lo < NS - 1 < hi or g is None:
                        dve.wait_ge(ssx_ready, n + 1)
                    dve.tensor_scalar(ms[:, nslot, lo:hi], ss[:, nslot, lo:hi], 1.0 / DH, RMS_EPS,
                                      ALU.mult, ALU.add).then_inc(ms_ready, 1)
                d = group(base, u, LAG_OUT)
                if d is not None:
                    slot = (u - LAG_OUT) % 2
                    dve.wait_ge(w_ps, d + 1)
                    if later(d, 2):
                        dve.wait_ge(x2T_ps, d - 1)
                    dve.tensor_tensor(x2[:, slot, :], p_w[:, 0:D], x_in[:, d, :], ALU.add).then_inc(x2_ready, 1)
                if n is not None:
                    y0, a, b = rs0[:, nslot, lo:hi], newton_a[:, nslot, lo:hi], newton_b[:, nslot, lo:hi]
                    dve.wait_ge(rs0_ready, n + 1)
                    dve.scalar_tensor_tensor(out=a, in0=y0, scalar=-0.5, in1=y0, op0=ALU.mult,
                                             op1=ALU.mult).then_inc(newton_step, 1)
                    dve.wait_ge(newton_step, 2 * n + 1)
                    dve.tensor_tensor(b, a, ms[:, nslot, lo:hi], ALU.mult).then_inc(newton_step, 1)
                    dve.wait_ge(newton_step, 2 * n + 2)
                    if later(n, 2) and n_has_x(n - 2):
                        dve.wait_ge(xhat_ready, n - 1)
                    dve.scalar_tensor_tensor(out=rs[:, nslot, lo:hi], in0=b, scalar=1.5, in1=y0, op0=ALU.add,
                                             op1=ALU.mult).then_inc(rs_ready, 1)
                if g is not None:
                    slot = (u - LAG_QKV) % 2
                    dve.wait_ge(rs_ready, n + 1)
                    if later(g, 2):
                        dve.wait_ge(qkT_ps, g - 1)
                    dve.tensor_tensor(qkn[:, slot, :].rearrange("p (h d) -> p h d", d=DH),
                                      p_qk[:, :].rearrange("p (h d) -> p h d", d=DH),
                                      rs[:, nslot, 0:2 * HEADS].unsqueeze(2).broadcast_to([P, 2 * HEADS, DH]),
                                      ALU.mult).then_inc(qkn_ready, 1)
                g = group(base, u, LAG_PV)
                if g is not None:
                    slot = (u - LAG_PV) % 2
                    o_heads = p_o[:, 0:GB * HEADS // 4 * VW].rearrange("p (n f) -> p n f", f=VW)
                    dve.wait_ge(o_ps, g + 1)
                    dve.reciprocal(inv_sum[:, slot, :], o_heads[:, :, DH]).then_inc(inv_ready, 1)
                    dve.wait_ge(inv_ready, g + 1)
                    dve.tensor_tensor(o_sb[:, slot, :].rearrange("p (n d) -> p n d", d=DH), o_heads[:, :, 0:DH],
                                      inv_sum[:, slot, :].unsqueeze(2).broadcast_to([P, HEADS, DH]),
                                      ALU.mult).then_inc(o_ready, 1)
                    dve.wait_ge(o_ready, g + 1)
                    if later(g, 2):
                        dve.wait_ge(oT_lo_ready, g - 1)
                    dve.transpose(oT[:, slot, :], o_sb[:, slot, :]).then_inc(oT_ready, 1)
                if isinstance(base, int) and base + u == LAG_QKV:
                    output_weights()
                if isinstance(base, int) and base + u == LAG_QKV + 1:
                    gru_biases()

            def n_has_x(n):
                return not isinstance(n, int) or n < NG

            pipeline(dve, body, NG - 1 + LAG_OUT)

            def step(base, s):
                t = base + s
                pair_slot, e = s // 2, s % 2
                for c in range(KC):
                    xnh = gru_bank(pair_slot, c, 1)
                    dve.wait_ge(r_ready[c], t + 1)
                    dve.scalar_tensor_tensor(out=rh[:, c, :], in0=xnh[:, HN_COL:HN_COL + B],
                                             scalar=bhh[:, 2 * KC + c:2 * KC + c + 1], in1=r_g[:, c, :],
                                             op0=ALU.add, op1=ALU.mult).then_inc(rh_ready[c], 1)
                    dve.wait_ge(rh_ready[c], t + 1)
                    dve.tensor_tensor(npre[:, c, :], xnh[:, IN_COL + e * B:IN_COL + e * B + B], rh[:, c, :],
                                      ALU.add).then_inc(npre_ready[c], 1)
                    dve.wait_ge(n_ready[c], t + 1)
                    dve.tensor_tensor(zn[:, c, :], omz[:, c, :], n_g[:, c, :], ALU.mult).then_inc(zn_ready[c], 1)
                    dve.wait_ge(zn_ready[c], t + 1)
                    dve.wait_ge(zh_ready[c], t + 1)
                    if later(t, 2):
                        dve.wait_ge(yT_ready, t - 1)
                    dve.tensor_tensor(h[:, s % 2, c, :], zn[:, c, :], zh[:, c, :], ALU.add).then_inc(h_ready[c], 1)

            gru_steps(dve, step)

        @block.tensor
        def _(pe):
            def products(dst, hi, lo, whi, wlo, start=True):
                terms = [(a[c], w[c]) for c in range(KC) for a, w in ((hi, whi), (hi, wlo), (lo, whi))]
                for i, (a, w) in enumerate(terms):
                    last = pe.matmul(dst, a, w, start=start and i == 0, stop=i == len(terms) - 1,
                                     skip_group_check=True)
                return last

            pe.wait_ge(ident_ready, 1)
            pe.wait_ge(vec_loaded, 16 * 6)
            pe.transpose(p_o[:, 0:20], vec_rows[:, :], ident[0:20, 0:20]).then_inc(vec_ps, 1)
            pe.wait_ge(cond_loaded, 16)
            for c in range(KC):
                last = pe.transpose(p_w[:, c * B:c * B + B], cond_sb[:, c * P:c * P + P], ident[:, :])
            last.then_inc(condT_ps, 1)
            pe.wait_ge(condT_ready, 1)
            pe.wait_ge(emb_loaded, 16)
            for m in range(2 * KC):
                for c in range(KC):
                    last = pe.matmul(p_s[:, m * B:m * B + B], w_emb_sb[:, c, m * P:m * P + P], h[:, 1, c, :],
                                     start=c == 0, stop=c == KC - 1)
            last.then_inc(emb_ps, 1)

            def body(base, u):
                g = group(base, u, LAG_QKV)
                if g is not None:
                    slot = (u - LAG_QKV) % 2
                    hi = [xn_hi[:, slot, c * P:c * P + P] for c in range(KC)]
                    lo = [xn_lo[:, slot, c * P:c * P + P] for c in range(KC)]
                    pe.wait_ge(xn_lo_ready, g + 1)
                    if isinstance(g, int) and g == 0:
                        pe.wait_ge(wqkv_ready, 1)
                    if later(g, 1):
                        pe.wait_ge(qkn_ready, g)
                    products(p_qk[:, :], hi, lo, [wqkv_hi[:, c, 0:2 * D] for c in range(KC)],
                             [wqkv_lo[:, c, 0:2 * D] for c in range(KC)]).then_inc(qk_ps, 1)
                    if later(g, 1):
                        pe.wait_ge(v_ready, g)
                    products(p_v[:, 0:D], hi, lo, [wqkv_hi[:, c, 2 * D:3 * D] for c in range(KC)],
                             [wqkv_lo[:, c, 2 * D:3 * D] for c in range(KC)]).then_inc(v_ps, 1)
                g = group(base, u, LAG_MOD)
                if g is not None:
                    slot = (u - LAG_MOD) % 2
                    pe.wait_ge(xhat_ready, g + 1)
                    if later(g, 1):
                        pe.wait_ge(xmod_ready, g)
                    for c in range(KC):
                        last = pe.transpose(p_xT[:, c * P:c * P + P], xhat[:, slot, c * P:c * P + P], ident[:, :])
                    last.then_inc(xT_ps, 1)
                d = group(base, u, LAG_OUT)
                if d is not None:
                    slot = (u - LAG_OUT) % 2
                    pe.wait_ge(oT_lo_ready, d + 1)
                    if isinstance(d, int) and d == 0:
                        pe.wait_ge(wo_ready, 1)
                    if later(d, 1):
                        pe.wait_ge(x2_ready, d)
                    products(p_w[:, 0:D], [oT_hi[:, slot, c * P:c * P + P] for c in range(KC)],
                             [oT_lo[:, slot, c * P:c * P + P] for c in range(KC)],
                             [wo_hi[:, c, :] for c in range(KC)], [wo_lo[:, c, :] for c in range(KC)])\
                        .then_inc(w_ps, 1)
                g = group(base, u, LAG_PV)
                if g is not None:
                    pe.wait_ge(probsT_ready, g + 1)
                    pe.wait_ge(v_ready, g + 1)
                    if later(g, 1):
                        pe.wait_ge(o_ready, g)
                    for hq in range(HEADS // 4):
                        for j in range(4):
                            c, e = hq // 2, hq % 2
                            head = HC * c + 2 * j + e
                            dst = p_o[32 * j:32 * j + 32, 0:GB * HEADS // 4 * VW]\
                                .rearrange("p (b n f) -> p b n f", b=GB, f=VW)[:, :, hq, :]
                            last = pe.matmul(dst, probsT[:, (u - LAG_PV) % 2, head, :],
                                             v_diag[:, (u - LAG_PV) % 4, :, head, :], start=True, stop=True)
                    last.then_inc(o_ps, 1)
                g = group(base, u, LAG_S)
                if g is not None:
                    slot = (u - LAG_S) % 2
                    pe.wait_ge(k_diag_ready[slot], spread(g, slot))
                    pe.wait_ge(qT_ready, g + 1)
                    if later(g, 1):
                        pe.wait_ge(logits_ready, g)
                    for c in range(KC):
                        for b in range(GB):
                            last = pe.matmul(p_s[T * b:T * b + T, c * D:c * D + D],
                                             qT[:, (u - LAG_S) % 4, c * P + T * b:c * P + T * b + T],
                                             k_diag[:, (u - LAG_S) % 2, GB * c + b, :, :].rearrange("p h k -> p (h k)"),
                                             start=True, stop=True)
                    last.then_inc(s_ps, 1)
                g = group(base, u, LAG_QKV)
                if g is not None:
                    slot = (u - LAG_QKV) % 2
                    pe.wait_ge(qkn_ready, g + 1)
                    if later(g, 1):
                        pe.wait_ge(qT_ready, g)
                    for m in range(2 * KC):
                        last = pe.transpose(p_qkT[:, m * P:m * P + P], qkn[:, slot, m * P:m * P + P], ident[:, :])
                    last.then_inc(qkT_ps, 1)
                if d is not None:
                    slot = (u - LAG_OUT) % 2
                    pe.wait_ge(x2_ready, d + 1)
                    if later(d, 1):
                        pe.wait_ge(x2T_ready, d)
                    for c in range(KC):
                        last = pe.transpose(p_x2T[:, c * P:c * P + P], x2[:, slot, c * P:c * P + P], ident[:, :])
                    last.then_inc(x2T_ps, 1)

            pe.wait_ge(mod_ready, 1)
            pipeline(pe, body, NG - 1 + LAG_OUT)

            def gate(weights, name, c):
                col = "rzn".index(name) * D + c * P
                return [weights[:, k, col:col + P] for k in range(KC)]

            def input_gates(slot, c, part):
                xhi = [pair_hi[:, slot, k, :] for k in range(KC)]
                xlo = [pair_lo[:, slot, k, :] for k in range(KC)]
                for name, col in ((("r", R_COL), ("z", Z_COL)), (("n", IN_COL),))[part]:
                    whi, wlo = gate(wih_hi, name, c), gate(wih_lo, name, c)
                    dst = gru_bank(slot, c, part)[:, col:col + 2 * B]
                    products(dst, whi, wlo, xhi, xlo, start=name != "z")

            def state_gates(s, c, k):
                slot, e = s // 2, s % 2
                rz, xnh = gru_bank(slot, c, 0), gru_bank(slot, c, 1)
                moving = h[:, (s + 1) % 2, k, :]
                for name, dst in (("z", rz[:, Z_COL + e * B:Z_COL + e * B + B]), ("n", xnh[:, HN_COL:HN_COL + B]),
                                  ("r", rz[:, R_COL + e * B:R_COL + e * B + B])):
                    last = pe.matmul(dst, gate(w_hh_sb, name, c)[k], moving, start=name == "n" and k == 0,
                                     stop=k == KC - 1, skip_group_check=True)
                return last

            def output_transposes(t, s, slot):
                pe.wait_ge(yT_ready, t + 1)
                if later(t, 1):
                    pe.wait_ge(y_ready, t)
                for c in range(KC):
                    last = pe.transpose(gru_bank(slot, c, 1)[:, SPARE_COL:SPARE_COL + P], yT[:, s % 2, c, :],
                                        ident[:, :])
                last.then_inc(y_ps, 1)

            pe.wait_ge(pair_lo_ready, 1)
            pe.wait_ge(x2T_ready, NG)
            pe.wait_ge(wih_ready, 1)
            pe.wait_ge(hh_loaded, 16)
            for c in range(KC):
                for part in range(2):
                    input_gates(0, c, part)

            def step(base, s):
                t = base + s
                slot, e = s // 2, s % 2
                if later(t, 1):
                    pe.wait_ge(h_ready[0], t)
                state_gates(s, 0, 0)
                if later(t, 1):
                    pe.wait_ge(h_ready[1], t)
                state_gates(s, 0, 1).then_inc(gates_ps[0], 1)
                state_gates(s, 1, 0)
                state_gates(s, 1, 1).then_inc(gates_ps[1], 1)
                if later(t, 1):
                    output_transposes(t - 1, (s - 1) % 4, 1 - slot)
                if has_pair(base, s // 2 + 1):
                    pe.wait_ge(pair_lo_ready, pair_index(base, s // 2 + 1) + 1)
                    input_gates(1 - slot, e, 0)
                    if later(t, 1):
                        pe.wait_ge(y_ready, t)
                    input_gates(1 - slot, e, 1)

            gru_steps(pe, step)
            output_transposes(T - 1, 3, 0)


_INS = ['x', 'cond_2048', 'L0_cond_W_emb', 'L0_cond_b_emb', 'L0_cond_g_norm', 'L0_cond_W_qkv', 'L0_cond_g_q',
        'L0_cond_g_k', 'L0_cond_W_out', 'L1_cond_W_ih', 'L1_cond_W_hh', 'L1_cond_b_ih', 'L1_cond_b_hh']
_OUTS = [((B, T, D), 'float32')]


def kernel(**inputs):
    import numpy as _np
    import concourse.bacc as _bacc
    from concourse import mybir as _mybir
    from concourse.bass_utils import run_bass_kernel_spmd as _run

    nc = _bacc.Bacc("TRN2", target_bir_lowering=False, num_devices=1)
    arrays, args = {}, []
    for name in _INS:
        a = _np.ascontiguousarray(inputs[name])
        arrays[f"in_{name}_dram"] = a
        args.append(nc.dram_tensor(f"in_{name}_dram", a.shape, _mybir.dt.from_np(a.dtype), kind="ExternalInput").ap())
    for i, (shape, dtype) in enumerate(_OUTS):
        dt = _mybir.dt.from_np(_np.dtype(dtype))
        args.append(nc.dram_tensor(f"out_{i}_dram", shape, dt, kind="ExternalOutput").ap())
    adaptive_attention_gru(nc, *args)
    r = _run(nc, [arrays], core_ids=[0])
    return r.results[0]["out_0_dram"]
```

```python
from contextlib import ExitStack

import concourse.bass as bass
from concourse import mybir

F32 = mybir.dt.float32
F32R = mybir.dt.float32r
ALU = mybir.AluOpType
ACT = mybir.ActivationFunctionType
AX_X = mybir.AxisListType.X

P = 128
B, T, D = 128, 32, 256
HEADS, DH = 16, 16
KC = D // P
GB = P // T
NG = B // GB
HC = HEADS // KC
BANK = 512
VW = DH + 1
RMS_EPS = 1e-6

LAG_X = 0
LAG_MOD = 1
LAG_QK = 2
LAG_V = LAG_QKT = 3
LAG_S = 5
LAG_PV = 6
LAG_OUT = 7
LAG_X2T = 8
UNROLL = 4
FIRST_LOOPED = 12


def adaptive_attention_gru(
    nc: bass.Bass, x, cond, w_emb, b_emb, g_norm, w_qkv, g_q, g_k, w_out, w_ih, w_hh, b_ih, b_hh, out,
):
    ctx = ExitStack()
    with ctx:
        def sb(name, shape, dt=F32):
            return ctx.enter_context(nc.sbuf_tensor(name, shape, dt))

        def bank(name):
            return ctx.enter_context(nc.psum_tensor(name, [P, BANK], F32))

        def sem(name):
            return ctx.enter_context(nc.semaphore(name))

        ident = sb("ident", [P, P])
        stage_w = sb("stage_w", [P, KC, 3 * D])
        stage_wo = sb("stage_wo", [P, KC, D])
        w_emb_sb = sb("w_emb_sb", [P, KC, 2 * D])
        w_hh_sb = sb("w_hh_sb", [P, KC, 3 * D])
        wqkv_hi = sb("wqkv_hi", [P, KC, 3 * D], F32R)
        wqkv_lo = sb("wqkv_lo", [P, KC, 3 * D], F32R)
        wo_hi = sb("wo_hi", [P, KC, D], F32R)
        wo_lo = sb("wo_lo", [P, KC, D], F32R)
        wih_hi = sb("wih_hi", [P, KC, 3 * D], F32R)
        wih_lo = sb("wih_lo", [P, KC, 3 * D], F32R)
        cond_sb = sb("cond_sb", [P, D])
        vec_rows = sb("vec_rows", [20, P])
        vec_cols = sb("vec_cols", [P, 20])
        bih, bhh = vec_cols[:, 0:6], vec_cols[:, 6:12]
        bemb = vec_cols[:, 12:16]
        gnorm = vec_cols[:, 16:18]
        gq_col, gk_col = vec_cols[:, 18:19], vec_cols[:, 19:20]
        bemb1 = sb("bemb1", [P, KC])
        gqk = sb("gqk", [P, 1])
        bsum = sb("bsum", [P, 4])
        bneg = sb("bneg", [P, 4])
        mod_scale = sb("mod_scale", [P, KC, NG, GB])
        mod_shift = sb("mod_shift", [P, KC, NG, GB])
        h = sb("h", [P, 2, KC, B])

        x_in = sb("x_in", [P, NG, D])
        square_x = sb("square_x", [P, D])
        xhat = sb("xhat", [P, 2, D])
        xmod = sb("xmod", [P, 2, D])
        xn = sb("xn", [P, 2, D])
        xn_hi = sb("xn_hi", [P, 2, D], F32R)
        xn_lo = sb("xn_lo", [P, 2, D], F32R)
        NS = 2 * HEADS + 1
        square_qk = sb("square_qk", [P, 2 * D])
        ss = sb("ss", [P, 2, NS])
        ms4 = sb("ms4", [P, 2, NS])
        threes = sb("threes", [P, NS])
        ln_ms = sb("ln_ms", [P, 2, NS])
        rs0 = sb("rs0", [P, 2, NS])
        newton_a = sb("newton_a", [P, 2, NS])
        newton_b = sb("newton_b", [P, 2, NS])
        rs = sb("rs", [P, 2, NS])
        qkn = sb("qkn", [P, 2, 2 * D])
        kT = sb("kT", [P, 2, D])
        qT = sb("qT", [P, 4, D])
        k_diag = sb("k_diag", [P, 2, KC * GB, HC, T])
        v_diag = sb("v_diag", [P, 4, GB, HEADS, VW])
        row_max = sb("row_max", [P, 2, HEADS])
        logits = sb("logits", [P, 2, HEADS * T])
        probs = sb("probs", [P, 2, HEADS * T])
        probsT = sb("probsT", [P, 2, HEADS, T])
        inv_sum = sb("inv_sum", [P, 2, HEADS])
        o_sb = sb("o_sb", [P, 2, D])
        oT = sb("oT", [P, 2, D])
        oT_hi = sb("oT_hi", [P, 2, D], F32R)
        oT_lo = sb("oT_lo", [P, 2, D], F32R)
        x2 = sb("x2", [P, 2, D])
        x2T = sb("x2T", [P, KC * T * B])

        pair_hi = sb("pair_hi", [P, 2, KC, 2 * B], F32R)
        pair_lo = sb("pair_lo", [P, 2, KC, 2 * B], F32R)
        freed = k_diag[:, :, :, :, :].rearrange("p s j h k -> p (s j h k)")
        taken = [0]

        def gru_tile(*shape):
            n = 1
            for size in shape:
                n *= size
            flat = freed[:, taken[0]:taken[0] + n]
            taken[0] += n
            names = " ".join("abc"[:len(shape)])
            sizes = {k: v for k, v in zip("abc", shape)}
            return flat.rearrange(f"p ({names}) -> p {names}", **sizes)

        r_g, z_g, omz, rh, npre, n_g, zh, zn = (gru_tile(KC, B) for _ in range(8))
        yT = gru_tile(2, KC, B)
        y_out = gru_tile(2, 2, D)

        banks = [bank(f"bank{i}") for i in range(8)]
        p_xT, p_vx2, p_qkT, p_s, p_o, p_w = banks[0:6]
        p_qk = banks[6:8]
        p_x2T, p_v = p_vx2[:, 0:D], p_vx2[:, D:2 * D]

        x_loaded = [sem(f"x_loaded{i}") for i in range(8)]
        cond_loaded = sem("cond_loaded")
        emb_loaded = sem("emb_loaded")
        vec_loaded = sem("vec_loaded")
        qkv_loaded = sem("qkv_loaded")
        wo_loaded = sem("wo_loaded")
        ih_loaded = sem("ih_loaded")
        hh_loaded = sem("hh_loaded")
        ident_zero = sem("ident_zero")
        ident_ready = sem("ident_ready")
        condT_ps = sem("condT_ps")
        condT_ready = sem("condT_ready")
        emb_ps = sem("emb_ps")
        vec_ps = sem("vec_ps")
        vec_cols_ready = sem("vec_cols_ready")
        vec_ready = sem("vec_ready")
        mod_ready = sem("mod_ready")
        diag_clear = sem("diag_clear")
        ones_ready = sem("ones_ready")
        wqkv_hi_ready = sem("wqkv_hi_ready")
        wqkv_ready = sem("wqkv_ready")
        wo_sum = sem("wo_sum")
        wo_hi_ready = sem("wo_hi_ready")
        wo_ready = sem("wo_ready")
        wih_hi_ready = sem("wih_hi_ready")
        wih_ready = sem("wih_ready")
        gru_bias = sem("gru_bias")
        gru_bias_ready = sem("gru_bias_ready")

        threes_ready = sem("threes_ready")

        ssx_ready = sem("ssx_ready")
        ssqk_ready = sem("ssqk_ready")
        ms4_ready = sem("ms4_ready")
        ln_ready = sem("ln_ready")
        rs0_ready = sem("rs0_ready")
        newton_step = sem("newton_step")
        rs_ready = sem("rs_ready")
        xhat_ready = sem("xhat_ready")
        xT_ps = sem("xT_ps")
        xmod_ready = sem("xmod_ready")
        xn_ready = sem("xn_ready")
        xn_hi_ready = sem("xn_hi_ready")
        xn_lo_ready = sem("xn_lo_ready")
        qk_ps = sem("qk_ps")
        v_ps = sem("v_ps")
        sq_ready = sem("sq_ready")
        qkn_ready = sem("qkn_ready")
        v_ready = sem("v_ready")
        qkT_ps = sem("qkT_ps")
        kT_ready = sem("kT_ready")
        qT_ready = sem("qT_ready")
        k_diag_ready = [sem("k_diag_ready0"), sem("k_diag_ready1")]
        s_ps = sem("s_ps")
        max_ready = sem("max_ready")
        logits_ready = sem("logits_ready")
        probs_ready = sem("probs_ready")
        probsT_ready = sem("probsT_ready")
        o_ps = sem("o_ps")
        inv_ready = sem("inv_ready")
        o_ready = sem("o_ready")
        oT_ready = sem("oT_ready")
        oT_hi_ready = sem("oT_hi_ready")
        oT_lo_ready = sem("oT_lo_ready")
        w_ps = sem("w_ps")
        x2_ready = sem("x2_ready")
        x2T_ps = sem("x2T_ps")
        x2T_ready = sem("x2T_ready")

        gates_ps = [sem(f"gates_ps{c}") for c in range(KC)]
        r_ready = [sem(f"r_ready{c}") for c in range(KC)]
        z_ready = [sem(f"z_ready{c}") for c in range(KC)]
        omz_ready = [sem(f"omz_ready{c}") for c in range(KC)]
        rh_ready = [sem(f"rh_ready{c}") for c in range(KC)]
        npre_ready = [sem(f"npre_ready{c}") for c in range(KC)]
        n_ready = [sem(f"n_ready{c}") for c in range(KC)]
        zh_ready = [sem(f"zh_ready{c}") for c in range(KC)]
        zn_ready = [sem(f"zn_ready{c}") for c in range(KC)]
        h_ready = [sem(f"h_ready{c}") for c in range(KC)]
        pair_hi_ready = sem("pair_hi_ready")
        pair_lo_ready = sem("pair_lo_ready")
        yT_ready = sem("yT_ready")
        y_ps = sem("y_ps")
        y_ready = sem("y_ready")
        out_done = [sem("out_done0"), sem("out_done1")]

        def group(base, u, lag, count=NG):
            g = base + (u - lag)
            if isinstance(g, int) and not 0 <= g < count:
                return None
            return g

        def later(g, n):
            return not isinstance(g, int) or g >= n

        def spread(g, slot):
            return (g - slot) * (8 * HC) + 16 * HC

        def pipeline(eng, body, last):
            for i in range(FIRST_LOOPED):
                body(i - i % UNROLL, i % UNROLL)
            with eng.Fori(FIRST_LOOPED // UNROLL, NG // UNROLL) as q:
                for u in range(UNROLL):
                    body(q * UNROLL, u)
            for i in range(NG, last + 1):
                body(i - i % UNROLL, i % UNROLL)

        def norm_columns(n):
            if isinstance(n, int):
                return (0 if n >= LAG_QK else NS - 1), (NS if n < NG else NS - 1)
            return 0, NS

        def gru_bank(pair_slot, chunk, part):
            return banks[4 * pair_slot + 2 * chunk + part]

        def pair_index(base, n):
            return (base // 4) * 2 + n if isinstance(base, int) else turn[0] * 2 + n

        def has_pair(base, n):
            return not isinstance(base, int) or base // 2 + n < T // 2

        def x2T_pair(u):
            return x2T[:, :].rearrange("p (c u n) -> p c u n", c=KC, n=2 * B)[:, :, u, :]

        turn = [0]

        def gru_steps(eng, body):
            for s in range(4):
                body(0, s)
            with eng.Fori(1, T // 4 - 1) as q:
                turn[0] = q
                for s in range(4):
                    body(q * 4, s)
            for s in range(4):
                body(T - 4, s)

        R_COL, Z_COL, IN_COL, HN_COL, SPARE_COL = 0, 2 * B, 0, 2 * B, 3 * B

        block = ctx.enter_context(nc.Block())

        @block.sync
        def _(sp):
            x_groups = x.rearrange("(g b) t d -> (b t) g d", b=GB)

            def load_x(i):
                n = NG // len(x_loaded)
                sp.dma_start(x_in[:, n * i:n * i + n, :], x_groups[:, n * i:n * i + n, :]).then_inc(x_loaded[i], 16)

            sp.dma_start(cond_sb[:, :], cond).then_inc(cond_loaded, 16)
            load_x(0)
            sp.dma_start(stage_w[:, :, :], w_qkv.rearrange("(c p) n -> p c n", p=P)).then_inc(qkv_loaded, 16)
            load_x(1)
            sp.dma_start(stage_wo[:, :, :], w_out.rearrange("(c p) n -> p c n", p=P)).then_inc(wo_loaded, 16)
            load_x(2)
            sp.dma_start(w_hh_sb[:, :, :], w_hh.rearrange("(c p) n -> p c n", p=P)).then_inc(hh_loaded, 16)
            for i in range(3, len(x_loaded)):
                load_x(i)
            sp.wait_ge(wqkv_ready, 1)
            sp.dma_start(stage_w[:, :, :], w_ih.rearrange("(c p) n -> p c n", p=P)).then_inc(ih_loaded, 16)

            sp.wait_ge(ones_ready, 1)

            def body(base, u):
                g = group(base, u, LAG_QKT)
                if g is not None:
                    slot = (u - LAG_QKT) % 2
                    sp.wait_ge(kT_ready, g + 1)
                    for hd in range(HC):
                        rows = slice(DH * hd, DH * hd + DH)
                        sp.dma_start(k_diag[rows, slot, :, hd, :],
                                     kT[rows, slot, :].rearrange("p (j k) -> p j k", k=T)).then_inc(k_diag_ready[slot], 16)

            pipeline(sp, body, NG - 1 + LAG_QKT)

            with sp.Fori(0, T // 4) as q:
                for slot in range(2):
                    sp.wait_ge(y_ready, q * 4 + 2 * slot + 2)
                    sp.wait_ge(x2T_ready, NG)
                    sp.dma_start(out[:, :, :].rearrange("b (u e) d -> b u (e d)", e=2)[:, q * 2 + slot, :],
                                 y_out[:, slot, :, :].rearrange("p e d -> p (e d)")).then_inc(out_done[slot], 16)
            for slot in range(2):
                sp.wait_ge(out_done[slot], 16 * (T // 4))

        @block.gpsimd
        def _(pool):
            pool.memset(ident[:, :], 0.0).then_inc(ident_zero, 1)
            pool.wait_ge(ident_zero, 1)
            pool.affine_select(out=ident[:, :], in_=ident[:, :], compare_op=ALU.not_equal, fill=1.0, base=0,
                               pattern=[[-1, P]], channel_multiplier=1).then_inc(ident_ready, 1)

            LATE_WEIGHTS = NG

            def split_late_weights():
                pool.wait_ge(ih_loaded, 16)
                pool.tensor_copy(wih_hi[:, :, :], stage_w[:, :, :]).then_inc(wih_hi_ready, 1)
                pool.wait_ge(wih_hi_ready, 1)
                pool.tensor_tensor(wih_lo[:, :, :], stage_w[:, :, :], wih_hi[:, :, :].bitcast(F32),
                                   ALU.subtract).then_inc(wih_ready, 1)

            def body(base, u):
                g = group(base, u, LAG_MOD)
                if g is not None:
                    slot = (u - LAG_MOD) % 2
                    shift = mod_shift[:, :, g, :].unsqueeze(3).broadcast_to([P, KC, GB, T])
                    pool.wait_ge(xmod_ready, g + 1)
                    if later(g, 2):
                        pool.wait_ge(xn_lo_ready, g - 1)
                    pool.tensor_tensor(xn[:, slot, :].rearrange("p (c b t) -> p c b t", c=KC, b=GB),
                                       xmod[:, slot, :].rearrange("p (c b t) -> p c b t", c=KC, b=GB),
                                       shift, ALU.add).then_inc(xn_ready, 1)
                o = group(base, u, LAG_OUT)
                if o is not None:
                    slot = (u - LAG_OUT) % 2
                    pool.wait_ge(oT_hi_ready, o + 1)
                    if later(o, 2):
                        pool.wait_ge(w_ps, o - 1)
                    pool.tensor_tensor(oT_lo[:, slot, :].rearrange("p (c b t) -> p b c t", c=KC, b=GB),
                                       oT[:, slot, :].rearrange("p (b c t) -> p b c t", c=KC, b=GB),
                                       oT_hi[:, slot, :].bitcast(F32).rearrange("p (c b t) -> p b c t", c=KC, b=GB),
                                       ALU.subtract).then_inc(oT_lo_ready, 1)
                if g is not None:
                    slot = (u - LAG_MOD) % 2
                    pool.wait_ge(xn_hi_ready, g + 1)
                    if later(g, 2):
                        pool.wait_ge(v_ps, g - 1)
                    pool.tensor_tensor(xn_lo[:, slot, :], xn[:, slot, :], xn_hi[:, slot, :].bitcast(F32),
                                       ALU.subtract).then_inc(xn_lo_ready, 1)
                n = group(base, u, LAG_X, NG + LAG_QK)
                if n is not None:
                    nslot = u % 2
                    lo, hi = norm_columns(n)
                    y0, a, b = rs0[:, nslot, lo:hi], newton_a[:, nslot, lo:hi], newton_b[:, nslot, lo:hi]
                    pool.wait_ge(rs0_ready, n + 1)
                    pool.tensor_tensor(a, y0, y0, ALU.mult).then_inc(newton_step, 1)
                    pool.wait_ge(newton_step, 3 * n + 1)
                    pool.tensor_tensor(b, a, ms4[:, nslot, lo:hi], ALU.mult).then_inc(newton_step, 1)
                    pool.wait_ge(newton_step, 3 * n + 2)
                    pool.tensor_tensor(a, threes[:, lo:hi], b, ALU.subtract).then_inc(newton_step, 1)
                    pool.wait_ge(newton_step, 3 * n + 3)
                    if later(n, 2):
                        pool.wait_ge(xhat_ready, min(n - 1, NG) if isinstance(n, int) else n - 1)
                        if later(n, 2 + LAG_QK):
                            pool.wait_ge(qkn_ready, n - 1 - LAG_QK)
                    pool.tensor_tensor(rs[:, nslot, lo:hi], a, y0, ALU.mult).then_inc(rs_ready, 1)
                if isinstance(base, int) and base + u == LATE_WEIGHTS:
                    split_late_weights()

            pool.memset(threes[:, :], 3.0).then_inc(threes_ready, 1)
            pool.wait_ge(threes_ready, 1)
            pool.wait_ge(mod_ready, 1)
            pipeline(pool, body, NG - 1 + LAG_OUT)
            pool.wait_ge(x2T_ready, NG)

            def split_pair(u, slot):
                pool.wait_ge(pair_hi_ready, u + 1)
                pool.tensor_tensor(pair_lo[:, slot, :, :], x2T_pair(u), pair_hi[:, slot, :, :].bitcast(F32),
                                   ALU.subtract).then_inc(pair_lo_ready, 1)

            split_pair(0, 0)
            split_pair(1, 1)

            def step(base, s):
                t = base + s
                for c in range(KC):
                    pool.wait_ge(z_ready[c], t + 1)
                    pool.tensor_tensor(zh[:, c, :], z_g[:, c, :], h[:, (s + 1) % 2, c, :],
                                       ALU.mult).then_inc(zh_ready[c], 1)
                pool.wait_ge(h_ready[0], t + 1)
                pool.wait_ge(h_ready[1], t + 1)
                if later(t, 2):
                    pool.wait_ge(y_ps, t - 1)
                pool.tensor_tensor(yT[:, s % 2, :, :], h[:, s % 2, :, :],
                                   x2T[:, :].rearrange("p (c t b) -> p c t b", c=KC, b=B)[:, :, t, :],
                                   ALU.add).then_inc(yT_ready, 1)
                if s % 2 == 0 and has_pair(base, s // 2 + 2):
                    split_pair(pair_index(base, s // 2 + 2), s // 2)

            gru_steps(pool, step)

        @block.scalar
        def _(act):
            act.dma_start(w_emb_sb[:, :, :], w_emb.rearrange("(c p) n -> p c n", p=P)).then_inc(emb_loaded, 16)
            for row, vector in ((0, b_ih), (6, b_hh), (12, b_emb), (16, g_norm)):
                n = vector.shape[0] // P
                act.dma_start(vec_rows[row:row + n, :], vector.rearrange("(n p) -> n p", p=P)).then_inc(vec_loaded, 16)
            for row, gain in ((18, g_q), (19, g_k)):
                act.dma_start(vec_rows[row:row + 1, :].rearrange("o (h d) -> o h d", d=DH),
                              gain.unsqueeze(0).unsqueeze(0).broadcast_to([1, HC, DH])).then_inc(vec_loaded, 16)
            act.preload_act_table_set("natural_log_exp_and_others")
            act.wait_ge(vec_ps, 1)
            act.copy(vec_cols[:, :], p_o[:, 0:20]).then_inc(vec_cols_ready, 1)
            act.wait_ge(condT_ps, 1)
            act.copy(h[:, 1, :, :], p_w[:, 0:KC * B].rearrange("p (c b) -> p c b", c=KC)).then_inc(condT_ready, 1)
            act.wait_ge(qkv_loaded, 16)
            act.copy(wqkv_hi[:, :, :], stage_w[:, :, :]).then_inc(wqkv_hi_ready, 1)

            def body(base, u):
                m = group(base, u, LAG_MOD)
                if m is not None:
                    act.wait_ge(rs_ready, m + 1)
                    if later(m, 2):
                        act.wait_ge(xT_ps, m - 1)
                n = group(base, u, LAG_X)
                nslot = u % 2
                if n is not None:
                    if isinstance(n, int):
                        if n % 4 == 0:
                            act.wait_ge(x_loaded[n // 4], 16)
                        if n == FIRST_LOOPED - 1:
                            for loaded in x_loaded[FIRST_LOOPED // 4:]:
                                act.wait_ge(loaded, 16)
                    if later(n, 2):
                        act.wait_ge(ms4_ready, n - 1)
                    if later(n, 1):
                        act.wait_ge(ssx_ready, n)
                g = group(base, u, LAG_PV)
                if g is not None:
                    slot = (u - LAG_PV) % 2
                    act.wait_ge(logits_ready, g + 1)
                    if later(g, 2):
                        act.wait_ge(probsT_ready, g - 1)
                    act.activation(probs[:, slot, :], logits[:, slot, :], ACT.Exp).then_inc(probs_ready, 1)
                if m is not None:
                    mslot = (u - LAG_MOD) % 2
                    act.activation(xhat[:, mslot, :], x_in[:, m, :], ACT.Copy,
                                   scale=rs[:, mslot, NS - 1:NS]).then_inc(xhat_ready, 1)
                if n is not None:
                    act.activation(square_x[:, :], x_in[:, n, :], ACT.Square, scale=(DH / D) ** 0.5,
                                   accum_out=ss[:, nslot, NS - 1:NS]).then_inc(ssx_ready, 1)
                g = group(base, u, LAG_QK)
                if g is not None:
                    act.wait_ge(qk_ps, g + 1)
                    if later(g, 1):
                        act.wait_ge(ssqk_ready, g)
                    act.activation(square_qk[:, :], p_qk[(u - LAG_QK) % 2][:, :], ACT.Square).then_inc(sq_ready, 1)
                g = group(base, u, LAG_OUT)
                if g is not None:
                    slot = (u - LAG_OUT) % 2
                    act.wait_ge(oT_ready, g + 1)
                    if later(g, 2):
                        act.wait_ge(w_ps, g - 1)
                    act.copy(oT_hi[:, slot, :].rearrange("p (c b t) -> p b c t", c=KC, b=GB),
                             oT[:, slot, :].rearrange("p (b c t) -> p b c t", c=KC, b=GB))\
                       .then_inc(oT_hi_ready, 1)

                def values(sequences):
                    for b in sequences:
                        rows = slice(T * b, T * b + T)
                        last = act.copy(v_diag[rows, (u - LAG_V) % 4, b, :, 0:DH],
                                        p_v[rows, :].rearrange("p (h d) -> p h d", h=HEADS))
                    return last

                v = group(base, u, LAG_V)
                if v is not None:
                    act.wait_ge(v_ps, v + 1)
                    if later(v, 4):
                        act.wait_ge(o_ps, v - 3)
                    if isinstance(v, int) and v == 0:
                        act.wait_ge(ones_ready, 2)
                d = group(base, u, LAG_X2T)
                if d is not None:
                    act.wait_ge(x2T_ps, d + 1)
                if v is not None:
                    values(range(0, 2))
                if d is not None:
                    act.copy(x2T[:, :].rearrange("p (c t g b) -> p c t g b", c=KC, t=T, b=GB)[:, :, :, d, :],
                             p_x2T.rearrange("p (c b t) -> p c t b", c=KC, b=GB)).then_inc(x2T_ready, 1)
                if m is not None:
                    slot = (u - LAG_MOD) % 2
                    act.wait_ge(xn_ready, m + 1)
                    if later(m, 2):
                        act.wait_ge(v_ps, m - 1)
                    act.copy(xn_hi[:, slot, :], xn[:, slot, :]).then_inc(xn_hi_ready, 1)
                n = group(base, u, LAG_X, NG + LAG_QK)
                if n is not None:
                    lo, hi = norm_columns(n)
                    act.wait_ge(ms4_ready, n + 1)
                    act.activation(ln_ms[:, nslot, lo:hi], ms4[:, nslot, lo:hi], ACT.Ln).then_inc(ln_ready, 1)
                    act.wait_ge(ln_ready, n + 1)
                    if later(n, 2):
                        act.wait_ge(rs_ready, n - 1)
                    act.activation(rs0[:, nslot, lo:hi], ln_ms[:, nslot, lo:hi], ACT.Exp,
                                   scale=-0.5).then_inc(rs0_ready, 1)
                if v is not None:
                    values(range(2, GB)).then_inc(v_ready, 1)
                g = group(base, u, LAG_QKT)
                if g is not None:
                    slot = (u - LAG_QKT) % 2
                    act.wait_ge(qkT_ps, g + 1)
                    if later(g, 2):
                        act.wait_ge(k_diag_ready[slot], spread(g - 2, slot))
                    act.copy(kT[:, slot, :], p_qkT[:, D:2 * D]).then_inc(kT_ready, 1)
                    if later(g, 4):
                        act.wait_ge(s_ps, g - 3)
                    act.activation(qT[:, (u - LAG_QKT) % 4, :], p_qkT[:, 0:D], ACT.Copy,
                                   scale=gqk[:, 0:1]).then_inc(qT_ready, 1)

            act.wait_ge(vec_ready, 1)
            pipeline(act, body, NG - 1 + LAG_X2T)

            act.preload_act_table(ACT.Sigmoid)
            act.wait_ge(gru_bias_ready, 1)
            act.wait_ge(x2T_ready, NG)

            def split_pair(u, slot):
                act.copy(pair_hi[:, slot, :, :], x2T_pair(u)).then_inc(pair_hi_ready, 1)

            split_pair(0, 0)
            split_pair(1, 1)

            def step(base, s):
                t = base + s
                pair_slot, e = s // 2, s % 2
                for c in range(KC):
                    rz, xnh = gru_bank(pair_slot, c, 0), gru_bank(pair_slot, c, 1)
                    r_in = rz[:, R_COL + e * B:R_COL + e * B + B]
                    z_in = rz[:, Z_COL + e * B:Z_COL + e * B + B]
                    act.wait_ge(gates_ps[c], t + 1)
                    act.activation(r_g[:, c, :], r_in, ACT.Sigmoid, bias=bsum[:, c:c + 1]).then_inc(r_ready[c], 1)
                    act.activation(z_g[:, c, :], z_in, ACT.Sigmoid,
                                   bias=bsum[:, KC + c:KC + c + 1]).then_inc(z_ready[c], 1)
                    act.activation(omz[:, c, :], z_in, ACT.Sigmoid, bias=bneg[:, KC + c:KC + c + 1],
                                   scale=-1.0).then_inc(omz_ready[c], 1)
                    act.wait_ge(npre_ready[c], t + 1)
                    act.activation(n_g[:, c, :], npre[:, c, :], ACT.Tanh,
                                   bias=bih[:, 2 * KC + c:2 * KC + c + 1]).then_inc(n_ready[c], 1)
                if e == 0 and has_pair(base, s // 2 + 2):
                    split_pair(pair_index(base, s // 2 + 2), s // 2)

            gru_steps(act, step)

        @block.vector
        def _(dve):
            dve.memset(k_diag[:, :, :, :, :], 0.0).then_inc(ones_ready, 1)
            dve.memset(v_diag[:, :, :, :, :], 0.0).then_inc(diag_clear, 1)
            dve.wait_ge(diag_clear, 1)
            for b in range(GB):
                last = dve.memset(v_diag[T * b:T * b + T, :, b, :, DH:VW], 1.0)
            last.then_inc(ones_ready, 1)
            dve.wait_ge(vec_cols_ready, 1)
            dve.scalar_tensor_tensor(out=gqk[:, :], in0=gq_col, scalar=DH ** -0.5, in1=gk_col,
                                     op0=ALU.mult, op1=ALU.mult).then_inc(vec_ready, 1)
            dve.tensor_scalar(bemb1[:, :], bemb[:, 0:KC], 1.0, None, ALU.add).then_inc(vec_ready, 1)
            dve.wait_ge(emb_ps, 1)
            dve.wait_ge(vec_ready, 2)
            for c in range(KC):
                dve.tensor_scalar(mod_scale[:, c, :, :].rearrange("p g b -> p (g b)"), p_s[:, c * B:c * B + B],
                                  bemb1[:, c:c + 1], gnorm[:, c:c + 1], ALU.add, ALU.mult)
            for c in range(KC):
                last = dve.tensor_scalar(mod_shift[:, c, :, :].rearrange("p g b -> p (g b)"),
                                         p_s[:, (KC + c) * B:(KC + c) * B + B], bemb[:, KC + c:KC + c + 1], None,
                                         ALU.add)
            last.then_inc(mod_ready, 1)
            dve.wait_ge(mod_ready, 1)
            dve.wait_ge(wqkv_hi_ready, 1)
            dve.tensor_tensor(wqkv_lo[:, :, :], stage_w[:, :, :], wqkv_hi[:, :, :].bitcast(F32),
                              ALU.subtract).then_inc(wqkv_ready, 1)

            def output_weights():
                dve.wait_ge(wo_loaded, 16)
                dve.wait_ge(ident_ready, 1)
                for c in range(KC):
                    last = dve.tensor_tensor(stage_wo[:, c, c * P:c * P + P], stage_wo[:, c, c * P:c * P + P],
                                             ident[:, :], ALU.add)
                last.then_inc(wo_sum, 1)
                dve.wait_ge(wo_sum, 1)
                dve.tensor_copy(wo_hi[:, :, :], stage_wo[:, :, :]).then_inc(wo_hi_ready, 1)
                dve.wait_ge(wo_hi_ready, 1)
                dve.tensor_tensor(wo_lo[:, :, :], stage_wo[:, :, :], wo_hi[:, :, :].bitcast(F32),
                                  ALU.subtract).then_inc(wo_ready, 1)

            def gru_biases():
                dve.tensor_tensor(bsum[:, :], bih[:, 0:2 * KC], bhh[:, 0:2 * KC], ALU.add).then_inc(gru_bias, 1)
                dve.wait_ge(gru_bias, 1)
                dve.tensor_scalar(bneg[:, :], bsum[:, :], -1.0, None, ALU.mult).then_inc(gru_bias_ready, 1)

            def body(base, u):
                o = group(base, u, LAG_OUT)
                if o is not None:
                    slot = (u - LAG_OUT) % 2
                    o_heads = p_o[:, 0:GB * HEADS // 4 * VW].rearrange("p (n f) -> p n f", f=VW)
                    dve.wait_ge(o_ps, o + 1)
                    dve.reciprocal(inv_sum[:, slot, :], o_heads[:, :, DH]).then_inc(inv_ready, 1)
                    dve.wait_ge(inv_ready, o + 1)
                    dve.tensor_tensor(o_sb[:, slot, :].rearrange("p (n d) -> p n d", d=DH), o_heads[:, :, 0:DH],
                                      inv_sum[:, slot, :].unsqueeze(2).broadcast_to([P, HEADS, DH]),
                                      ALU.mult).then_inc(o_ready, 1)
                g = group(base, u, LAG_PV)
                if g is not None:
                    slot = (u - LAG_PV) % 2
                    dve.wait_ge(probs_ready, g + 1)
                    if later(g, 2):
                        dve.wait_ge(o_ps, g - 1)
                    dve.transpose(probsT[:, slot, :, :].rearrange("p h q -> p (h q)"), probs[:, slot, :])\
                       .then_inc(probsT_ready, 1)
                if o is not None:
                    slot = (u - LAG_OUT) % 2
                    dve.wait_ge(o_ready, o + 1)
                    if later(o, 2):
                        dve.wait_ge(oT_lo_ready, o - 1)
                    dve.transpose(oT[:, slot, :], o_sb[:, slot, :]).then_inc(oT_ready, 1)
                g = group(base, u, LAG_MOD)
                if g is not None:
                    slot = (u - LAG_MOD) % 2
                    dve.wait_ge(xT_ps, g + 1)
                    if later(g, 2):
                        dve.wait_ge(xn_ready, g - 1)
                    dve.tensor_tensor(xmod[:, slot, :].rearrange("p (c b t) -> p c b t", c=KC, b=GB),
                                      p_xT[:, 0:D].rearrange("p (c b t) -> p c b t", c=KC, b=GB),
                                      mod_scale[:, :, g, :].unsqueeze(3).broadcast_to([P, KC, GB, T]),
                                      ALU.mult).then_inc(xmod_ready, 1)
                g = group(base, u, LAG_QKT)
                if g is not None:
                    slot = (u - LAG_QKT) % 2
                    dve.wait_ge(rs_ready, g + LAG_QK + 1)
                    if later(g, 2):
                        dve.wait_ge(qkT_ps, g - 1)
                    dve.tensor_tensor(qkn[:, slot, :].rearrange("p (h d) -> p h d", d=DH),
                                      p_qk[slot][:, :].rearrange("p (h d) -> p h d", d=DH),
                                      rs[:, (u - 1) % 2, 0:2 * HEADS].unsqueeze(2).broadcast_to([P, 2 * HEADS, DH]),
                                      ALU.mult).then_inc(qkn_ready, 1)
                g = group(base, u, LAG_QK)
                nslot = u % 2
                if g is not None:
                    dve.wait_ge(sq_ready, g + 1)
                    dve.tensor_reduce(ss[:, nslot, 0:2 * HEADS],
                                      square_qk[:, :].rearrange("p (h d) -> p h d", d=DH),
                                      AX_X, ALU.add).then_inc(ssqk_ready, 1)
                n = group(base, u, LAG_X, NG + LAG_QK)
                if n is not None:
                    lo, hi = norm_columns(n)
                    if g is not None:
                        dve.wait_ge(ssqk_ready, g + 1)
                    if lo < NS - 1 < hi or g is None:
                        dve.wait_ge(ssx_ready, n + 1)
                    if later(n, 2):
                        dve.wait_ge(rs_ready, n - 1)
                    dve.tensor_scalar(ms4[:, nslot, lo:hi], ss[:, nslot, lo:hi], 4.0 / DH, 4.0 * RMS_EPS,
                                      ALU.mult, ALU.add).then_inc(ms4_ready, 1)
                g = group(base, u, LAG_S)
                s_heads = p_s[:, :].rearrange("p (h k) -> p h k", h=HEADS)
                if g is not None:
                    slot = (u - LAG_S) % 2
                    dve.wait_ge(s_ps, g + 1)
                    dve.tensor_reduce(row_max[:, slot, :], s_heads, AX_X, ALU.max).then_inc(max_ready, 1)
                if o is not None:
                    slot = (u - LAG_OUT) % 2
                    dve.wait_ge(w_ps, o + 1)
                    if later(o, 2):
                        dve.wait_ge(x2T_ps, o - 1)
                    dve.tensor_tensor(x2[:, slot, :], p_w[:, 0:D], x_in[:, o, :], ALU.add).then_inc(x2_ready, 1)
                if g is not None:
                    slot = (u - LAG_S) % 2
                    dve.wait_ge(max_ready, g + 1)
                    if later(g, 2):
                        dve.wait_ge(probs_ready, g - 1)
                    dve.tensor_tensor(logits[:, slot, :].rearrange("p (h k) -> p h k", h=HEADS), s_heads,
                                      row_max[:, slot, :].unsqueeze(2).broadcast_to([P, HEADS, T]),
                                      ALU.subtract).then_inc(logits_ready, 1)
                if isinstance(base, int) and base + u == LAG_QK:
                    output_weights()
                if isinstance(base, int) and base + u == LAG_QK + 1:
                    gru_biases()

            pipeline(dve, body, NG - 1 + LAG_OUT)

            def store_step(t, s, pair_slot):
                dve.wait_ge(y_ps, t + 1)
                if s % 2 == 0 and later(t, 4):
                    dve.wait_ge(out_done[s // 2], (t - s) * 4)
                for c in range(KC):
                    last = dve.tensor_copy(y_out[:, s // 2, s % 2, c * P:c * P + P],
                                    gru_bank(pair_slot, c, 1)[:, SPARE_COL:SPARE_COL + P])
                last.then_inc(y_ready, 1)

            def step(base, s):
                t = base + s
                pair_slot, e = s // 2, s % 2
                for c in range(KC):
                    xnh = gru_bank(pair_slot, c, 1)
                    dve.wait_ge(r_ready[c], t + 1)
                    dve.scalar_tensor_tensor(out=rh[:, c, :], in0=xnh[:, HN_COL:HN_COL + B],
                                             scalar=bhh[:, 2 * KC + c:2 * KC + c + 1], in1=r_g[:, c, :],
                                             op0=ALU.add, op1=ALU.mult).then_inc(rh_ready[c], 1)
                    dve.wait_ge(rh_ready[c], t + 1)
                    dve.tensor_tensor(npre[:, c, :], xnh[:, IN_COL + e * B:IN_COL + e * B + B], rh[:, c, :],
                                      ALU.add).then_inc(npre_ready[c], 1)
                    if c == KC - 1 and later(t, 1):
                        store_step(t - 1, (s - 1) % 4, 1 - pair_slot)
                    dve.wait_ge(n_ready[c], t + 1)
                    dve.tensor_tensor(zn[:, c, :], omz[:, c, :], n_g[:, c, :], ALU.mult).then_inc(zn_ready[c], 1)
                    dve.wait_ge(zn_ready[c], t + 1)
                    dve.wait_ge(zh_ready[c], t + 1)
                    if later(t, 2):
                        dve.wait_ge(yT_ready, t - 1)
                    dve.tensor_tensor(h[:, s % 2, c, :], zn[:, c, :], zh[:, c, :], ALU.add).then_inc(h_ready[c], 1)

            gru_steps(dve, step)
            store_step(T - 1, 3, 0)

        @block.tensor
        def _(pe):
            def products(dst, hi, lo, whi, wlo, start=True):
                terms = [(a[c], w[c]) for c in range(KC) for a, w in ((hi, whi), (hi, wlo), (lo, whi))]
                for i, (a, w) in enumerate(terms):
                    last = pe.matmul(dst, a, w, start=start and i == 0, stop=i == len(terms) - 1,
                                     skip_group_check=True)
                return last

            pe.wait_ge(ident_ready, 1)
            pe.wait_ge(vec_loaded, 16 * 6)
            pe.transpose(p_o[:, 0:20], vec_rows[:, :], ident[0:20, 0:20]).then_inc(vec_ps, 1)
            pe.wait_ge(cond_loaded, 16)
            for c in range(KC):
                last = pe.transpose(p_w[:, c * B:c * B + B], cond_sb[:, c * P:c * P + P], ident[:, :])
            last.then_inc(condT_ps, 1)
            pe.wait_ge(condT_ready, 1)
            pe.wait_ge(emb_loaded, 16)
            for m in range(2 * KC):
                for c in range(KC):
                    last = pe.matmul(p_s[:, m * B:m * B + B], w_emb_sb[:, c, m * P:m * P + P], h[:, 1, c, :],
                                     start=c == 0, stop=c == KC - 1)
            last.then_inc(emb_ps, 1)

            def projection_input(u, lag):
                slot = (u - lag) % 2
                return ([xn_hi[:, slot, c * P:c * P + P] for c in range(KC)],
                        [xn_lo[:, slot, c * P:c * P + P] for c in range(KC)])

            def body(base, u):
                g = group(base, u, LAG_QK)
                if g is not None:
                    pe.wait_ge(xn_lo_ready, g + 1)
                    if isinstance(g, int) and g == 0:
                        pe.wait_ge(wqkv_ready, 1)
                    if later(g, 2):
                        pe.wait_ge(qkn_ready, g - 1)
                    hi, lo = projection_input(u, LAG_QK)
                    products(p_qk[(u - LAG_QK) % 2][:, :], hi, lo, [wqkv_hi[:, c, 0:2 * D] for c in range(KC)],
                             [wqkv_lo[:, c, 0:2 * D] for c in range(KC)]).then_inc(qk_ps, 1)
                g = group(base, u, LAG_MOD)
                if g is not None:
                    pe.wait_ge(xhat_ready, g + 1)
                    if later(g, 1):
                        pe.wait_ge(xmod_ready, g)
                    for c in range(KC):
                        last = pe.transpose(p_xT[:, c * P:c * P + P], xhat[:, (u - LAG_MOD) % 2, c * P:c * P + P],
                                            ident[:, :])
                    last.then_inc(xT_ps, 1)
                g = group(base, u, LAG_V)
                d = group(base, u, LAG_X2T)
                if not isinstance(base, int):
                    pe.wait_ge(v_ready, g)
                elif base + u > LAG_V:
                    pe.wait_ge(v_ready, min(base + u - LAG_V, NG))
                if d is not None:
                    if later(d, 1):
                        pe.wait_ge(x2T_ready, d)
                    pe.wait_ge(x2_ready, d + 1)
                    for c in range(KC):
                        last = pe.transpose(p_x2T[:, c * P:c * P + P], x2[:, (u - LAG_X2T) % 2, c * P:c * P + P],
                                            ident[:, :])
                    last.then_inc(x2T_ps, 1)
                if g is not None:
                    hi, lo = projection_input(u, LAG_V)
                    products(p_v, hi, lo, [wqkv_hi[:, c, 2 * D:3 * D] for c in range(KC)],
                             [wqkv_lo[:, c, 2 * D:3 * D] for c in range(KC)]).then_inc(v_ps, 1)
                g = group(base, u, LAG_S)
                if g is not None:
                    slot = (u - LAG_S) % 2
                    pe.wait_ge(k_diag_ready[slot], spread(g, slot))
                    pe.wait_ge(qT_ready, g + 1)
                    if later(g, 1):
                        pe.wait_ge(logits_ready, g)
                    for c in range(KC):
                        for b in range(GB):
                            last = pe.matmul(p_s[T * b:T * b + T, c * D:c * D + D],
                                             qT[:, (u - LAG_S) % 4, c * P + T * b:c * P + T * b + T],
                                             k_diag[:, slot, GB * c + b, :, :].rearrange("p h k -> p (h k)"),
                                             start=True, stop=True)
                    last.then_inc(s_ps, 1)
                g = group(base, u, LAG_QKT)
                if g is not None:
                    slot = (u - LAG_QKT) % 2
                    pe.wait_ge(qkn_ready, g + 1)
                    if later(g, 1):
                        pe.wait_ge(qT_ready, g)
                    for m in range(2 * KC):
                        last = pe.transpose(p_qkT[:, m * P:m * P + P], qkn[:, slot, m * P:m * P + P], ident[:, :])
                    last.then_inc(qkT_ps, 1)
                g = group(base, u, LAG_OUT)
                if g is not None:
                    slot = (u - LAG_OUT) % 2
                    pe.wait_ge(oT_lo_ready, g + 1)
                    if isinstance(g, int) and g == 0:
                        pe.wait_ge(wo_ready, 1)
                    if later(g, 1):
                        pe.wait_ge(x2_ready, g)
                    products(p_w[:, 0:D], [oT_hi[:, slot, c * P:c * P + P] for c in range(KC)],
                             [oT_lo[:, slot, c * P:c * P + P] for c in range(KC)],
                             [wo_hi[:, c, :] for c in range(KC)], [wo_lo[:, c, :] for c in range(KC)])\
                        .then_inc(w_ps, 1)
                g = group(base, u, LAG_PV)
                if g is not None:
                    pe.wait_ge(probsT_ready, g + 1)
                    pe.wait_ge(v_ready, g + 1)
                    if later(g, 1):
                        pe.wait_ge(o_ready, g)
                    for hq in range(HEADS // 4):
                        for j in range(4):
                            c, e = hq // 2, hq % 2
                            head = HC * c + 2 * j + e
                            dst = p_o[32 * j:32 * j + 32, 0:GB * HEADS // 4 * VW]\
                                .rearrange("p (b n f) -> p b n f", b=GB, f=VW)[:, :, hq, :]
                            last = pe.matmul(dst, probsT[:, (u - LAG_PV) % 2, head, :],
                                             v_diag[:, (u - LAG_PV) % 4, :, head, :], start=True, stop=True)
                    last.then_inc(o_ps, 1)

            pe.wait_ge(mod_ready, 1)
            pipeline(pe, body, NG - 1 + LAG_X2T)

            def gate(weights, name, c):
                col = "rzn".index(name) * D + c * P
                return [weights[:, k, col:col + P] for k in range(KC)]

            def input_gates(slot, c, part):
                xhi = [pair_hi[:, slot, k, :] for k in range(KC)]
                xlo = [pair_lo[:, slot, k, :] for k in range(KC)]
                for name, col in ((("r", R_COL), ("z", Z_COL)), (("n", IN_COL),))[part]:
                    whi, wlo = gate(wih_hi, name, c), gate(wih_lo, name, c)
                    dst = gru_bank(slot, c, part)[:, col:col + 2 * B]
                    products(dst, whi, wlo, xhi, xlo, start=name != "z")

            def state_gates(s, c, k):
                slot, e = s // 2, s % 2
                rz, xnh = gru_bank(slot, c, 0), gru_bank(slot, c, 1)
                moving = h[:, (s + 1) % 2, k, :]
                for name, dst in (("z", rz[:, Z_COL + e * B:Z_COL + e * B + B]), ("n", xnh[:, HN_COL:HN_COL + B]),
                                  ("r", rz[:, R_COL + e * B:R_COL + e * B + B])):
                    last = pe.matmul(dst, gate(w_hh_sb, name, c)[k], moving, start=name == "n" and k == 0,
                                     stop=k == KC - 1, skip_group_check=True)
                return last

            def output_transposes(t, s, slot):
                pe.wait_ge(yT_ready, t + 1)
                if later(t, 1):
                    pe.wait_ge(y_ready, t)
                for c in range(KC):
                    last = pe.transpose(gru_bank(slot, c, 1)[:, SPARE_COL:SPARE_COL + P], yT[:, s % 2, c, :],
                                        ident[:, :])
                last.then_inc(y_ps, 1)

            pe.wait_ge(pair_lo_ready, 1)
            pe.wait_ge(x2T_ready, NG)
            pe.wait_ge(wih_ready, 1)
            pe.wait_ge(hh_loaded, 16)
            for c in range(KC):
                for part in range(2):
                    input_gates(0, c, part)

            def step(base, s):
                t = base + s
                slot, e = s // 2, s % 2
                if later(t, 1):
                    pe.wait_ge(h_ready[0], t)
                state_gates(s, 0, 0)
                if later(t, 1):
                    pe.wait_ge(h_ready[1], t)
                state_gates(s, 0, 1).then_inc(gates_ps[0], 1)
                state_gates(s, 1, 0)
                state_gates(s, 1, 1).then_inc(gates_ps[1], 1)
                if later(t, 1):
                    output_transposes(t - 1, (s - 1) % 4, 1 - slot)
                if has_pair(base, s // 2 + 1):
                    pe.wait_ge(pair_lo_ready, pair_index(base, s // 2 + 1) + 1)
                    input_gates(1 - slot, e, 0)
                    if later(t, 1):
                        pe.wait_ge(y_ready, t)
                    input_gates(1 - slot, e, 1)

            gru_steps(pe, step)
            output_transposes(T - 1, 3, 0)


_INS = ['x', 'cond_2048', 'L0_cond_W_emb', 'L0_cond_b_emb', 'L0_cond_g_norm', 'L0_cond_W_qkv', 'L0_cond_g_q',
        'L0_cond_g_k', 'L0_cond_W_out', 'L1_cond_W_ih', 'L1_cond_W_hh', 'L1_cond_b_ih', 'L1_cond_b_hh']
_OUTS = [((B, T, D), 'float32')]


def kernel(**inputs):
    import numpy as _np
    import concourse.bacc as _bacc
    from concourse import mybir as _mybir
    from concourse.bass_utils import run_bass_kernel_spmd as _run

    nc = _bacc.Bacc("TRN2", target_bir_lowering=False, num_devices=1)
    arrays, args = {}, []
    for name in _INS:
        a = _np.ascontiguousarray(inputs[name])
        arrays[f"in_{name}_dram"] = a
        args.append(nc.dram_tensor(f"in_{name}_dram", a.shape, _mybir.dt.from_np(a.dtype), kind="ExternalInput").ap())
    for i, (shape, dtype) in enumerate(_OUTS):
        dt = _mybir.dt.from_np(_np.dtype(dtype))
        args.append(nc.dram_tensor(f"out_{i}_dram", shape, dt, kind="ExternalOutput").ap())
    adaptive_attention_gru(nc, *args)
    r = _run(nc, [arrays], core_ids=[0])
    return r.results[0]["out_0_dram"]
```

```python
from contextlib import ExitStack

import concourse.bass as bass
from concourse import mybir

F32 = mybir.dt.float32
F32R = mybir.dt.float32r
ALU = mybir.AluOpType
ACT = mybir.ActivationFunctionType
AX_X = mybir.AxisListType.X

P = 128
B, T, D = 128, 32, 256
HEADS, DH = 16, 16
KC = D // P
GB = P // T
NG = B // GB
HC = HEADS // KC
PB = 32
NB = P // PB
BANK = 512
VW = DH + 1
RMS_EPS = 1e-6

LAG_X = 0
LAG_HAT = 1
LAG_MOD = 2
LAG_QK = 3
LAG_V = LAG_QKT = 4
LAG_KEYS = 5
LAG_S = 6
LAG_PV = 7
LAG_OUT = 8
LAG_X2T = 9
UNROLL = 4
FIRST_NORMED = 4
FIRST_LOOPED = 12


def adaptive_attention_gru(
    nc: bass.Bass, x, cond, w_emb, b_emb, g_norm, w_qkv, g_q, g_k, w_out, w_ih, w_hh, b_ih, b_hh, out,
):
    ctx = ExitStack()
    with ctx:
        def sb(name, shape, dt=F32):
            return ctx.enter_context(nc.sbuf_tensor(name, shape, dt))

        def bank(name):
            return ctx.enter_context(nc.psum_tensor(name, [P, BANK], F32))

        def sem(name):
            return ctx.enter_context(nc.semaphore(name))

        ident = sb("ident", [P, P])
        stage_w = sb("stage_w", [P, KC, 3 * D])
        stage_wo = sb("stage_wo", [P, KC, D])
        w_emb_sb = sb("w_emb_sb", [P, KC, 2 * D])
        w_hh_sb = sb("w_hh_sb", [P, KC, 3 * D])
        wqkv_hi = sb("wqkv_hi", [P, KC, 3 * D], F32R)
        wqkv_lo = sb("wqkv_lo", [P, KC, 3 * D], F32R)
        wo_hi = sb("wo_hi", [P, KC, D], F32R)
        wo_lo = sb("wo_lo", [P, KC, D], F32R)
        wih_hi = sb("wih_hi", [P, KC, 3 * D], F32R)
        wih_lo = sb("wih_lo", [P, KC, 3 * D], F32R)
        cond_sb = sb("cond_sb", [P, D])
        vec_rows = sb("vec_rows", [20, P])
        vec_cols = sb("vec_cols", [P, 20])
        bih, bhh = vec_cols[:, 0:6], vec_cols[:, 6:12]
        bemb = vec_cols[:, 12:16]
        gnorm = vec_cols[:, 16:18]
        gq_col, gk_col = vec_cols[:, 18:19], vec_cols[:, 19:20]
        bemb1 = sb("bemb1", [P, KC])
        gqk = sb("gqk", [P, 1])
        head_rows = sb("head_rows", [P, P // DH])
        parity = sb("parity", [P, 2])
        gqk_parity = sb("gqk_parity", [P, 2])
        bsum = sb("bsum", [P, 4])
        bneg = sb("bneg", [P, 4])
        mod_scale = sb("mod_scale", [P, KC, NG, GB])
        mod_shift = sb("mod_shift", [P, KC, NG, GB])
        h = sb("h", [P, 2, KC, B])

        x_in = sb("x_in", [P, NG, D])
        square_x = sb("square_x", [P, D])
        xhat = sb("xhat", [P, 2, D])
        xmod = sb("xmod", [P, 2, D])
        xn = sb("xn", [P, 2, D])
        xn_hi = sb("xn_hi", [P, 2, D], F32R)
        xn_lo = sb("xn_lo", [P, 2, D], F32R)
        NS = 2 * HEADS + 1
        square_qk = sb("square_qk", [P, 2 * D])
        ss = sb("ss", [P, 2, NS])
        ms4 = sb("ms4", [P, 2, NS])
        threes = sb("threes", [P, NS])
        ln_ms = sb("ln_ms", [P, 2, NS])
        rs0 = sb("rs0", [P, 2, NS])
        newton_a = sb("newton_a", [P, 2, NS])
        newton_b = sb("newton_b", [P, 2, NS])
        rs = sb("rs", [P, 2, NS])
        norm_first = sb("norm_first", [P, 7, FIRST_NORMED])
        qkn = sb("qkn", [P, 2, 2 * D])
        qkT = sb("qkT", [P, 2, 2 * D])
        KD, KM = 2 * NB * 2 * D, 2 * 2 * D
        operands = sb("operands", [P, KD + KM])
        k_diag = operands[:, 0:KD].rearrange("p (s n r j k) -> p s n r j k", s=2, n=NB, r=2, k=T)
        k_masked = operands[:, KD:KD + KM].rearrange("p (s r f) -> p s r f", s=2, r=2)
        v_diag = sb("v_diag", [P, 4, GB, HEADS, VW])
        row_max = sb("row_max", [P, 2, HEADS])
        logits = sb("logits", [P, 2, HEADS * T])
        probs = sb("probs", [P, 2, HEADS * T])
        probsT = sb("probsT", [P, 2, HEADS, T])
        inv_sum = sb("inv_sum", [P, 2, HEADS])
        o_sb = sb("o_sb", [P, 2, D])
        oT = sb("oT", [P, 2, D])
        oT_hi = sb("oT_hi", [P, 2, D], F32R)
        oT_lo = sb("oT_lo", [P, 2, D], F32R)
        x2 = sb("x2", [P, 2, D])
        x2T = sb("x2T", [P, KC * T * B])

        pair_hi = sb("pair_hi", [P, 2, KC, 2 * B], F32R)
        pair_lo = sb("pair_lo", [P, 2, KC, 2 * B], F32R)
        taken = [0]

        def gru_tile(*shape):
            n = 1
            for size in shape:
                n *= size
            flat = operands[:, taken[0]:taken[0] + n]
            taken[0] += n
            names = " ".join("abc"[:len(shape)])
            sizes = {k: v for k, v in zip("abc", shape)}
            return flat.rearrange(f"p ({names}) -> p {names}", **sizes)

        r_g, z_g, omz, rh, npre, n_g, zh, zn = (gru_tile(KC, B) for _ in range(8))
        yT = gru_tile(2, KC, B)
        y_out = gru_tile(2, 2, D)

        banks = [bank(f"bank{i}") for i in range(8)]
        p_xT, p_vx2, p_qkT, p_s, p_o, p_w = banks[0:6]
        p_qk = banks[6:8]
        p_x2T, p_v = p_vx2[:, 0:D], p_vx2[:, D:2 * D]

        x_loaded = [sem(f"x_loaded{i}") for i in range(8)]
        cond_loaded = sem("cond_loaded")
        emb_loaded = sem("emb_loaded")
        vec_loaded = sem("vec_loaded")
        qkv_loaded = sem("qkv_loaded")
        wo_loaded = sem("wo_loaded")
        ih_loaded = sem("ih_loaded")
        hh_loaded = sem("hh_loaded")
        ident_zero = sem("ident_zero")
        ident_ready = sem("ident_ready")
        condT_ps = sem("condT_ps")
        condT_ready = sem("condT_ready")
        emb_ps = sem("emb_ps")
        vec_ps = sem("vec_ps")
        vec_cols_ready = sem("vec_cols_ready")
        vec_ready = sem("vec_ready")
        mod_ready = sem("mod_ready")
        k_diag_clear = sem("k_diag_clear")
        parity_step = sem("parity_step")
        v_diag_clear = sem("v_diag_clear")
        ones_ready = sem("ones_ready")
        wqkv_hi_ready = sem("wqkv_hi_ready")
        wqkv_ready = sem("wqkv_ready")
        wo_sum = sem("wo_sum")
        wo_hi_ready = sem("wo_hi_ready")
        wo_ready = sem("wo_ready")
        wih_hi_ready = sem("wih_hi_ready")
        wih_ready = sem("wih_ready")
        gru_bias = sem("gru_bias")
        gru_bias_ready = sem("gru_bias_ready")

        threes_ready = sem("threes_ready")

        ssx_ready = sem("ssx_ready")
        ssqk_ready = sem("ssqk_ready")
        ms4_ready = sem("ms4_ready")
        ln_ready = sem("ln_ready")
        rs0_ready = sem("rs0_ready")
        newton_step = sem("newton_step")
        rs_ready = sem("rs_ready")
        xhat_ready = sem("xhat_ready")
        xT_ps = sem("xT_ps")
        xmod_ready = sem("xmod_ready")
        xn_ready = sem("xn_ready")
        xn_hi_ready = sem("xn_hi_ready")
        xn_lo_ready = sem("xn_lo_ready")
        qk_ps = sem("qk_ps")
        v_ps = sem("v_ps")
        sq_ready = sem("sq_ready")
        qkn_ready = sem("qkn_ready")
        v_ready = sem("v_ready")
        qkT_ps = sem("qkT_ps")
        qkT_ready = sem("qkT_ready")
        k_masked_ready = sem("k_masked_ready")
        k_diag_ready = [sem("k_diag_ready0"), sem("k_diag_ready1")]
        s_ps = sem("s_ps")
        max_ready = sem("max_ready")
        logits_ready = sem("logits_ready")
        probs_ready = sem("probs_ready")
        probsT_ready = sem("probsT_ready")
        o_ps = sem("o_ps")
        inv_ready = sem("inv_ready")
        o_ready = sem("o_ready")
        oT_ready = sem("oT_ready")
        oT_hi_ready = sem("oT_hi_ready")
        oT_lo_ready = sem("oT_lo_ready")
        w_ps = sem("w_ps")
        x2_ready = sem("x2_ready")
        x2T_ps = sem("x2T_ps")
        x2T_ready = sem("x2T_ready")

        gates_ps = [sem(f"gates_ps{c}") for c in range(KC)]
        r_ready = [sem(f"r_ready{c}") for c in range(KC)]
        z_ready = [sem(f"z_ready{c}") for c in range(KC)]
        omz_ready = [sem(f"omz_ready{c}") for c in range(KC)]
        rh_ready = [sem(f"rh_ready{c}") for c in range(KC)]
        npre_ready = [sem(f"npre_ready{c}") for c in range(KC)]
        n_ready = [sem(f"n_ready{c}") for c in range(KC)]
        zh_ready = [sem(f"zh_ready{c}") for c in range(KC)]
        zn_ready = [sem(f"zn_ready{c}") for c in range(KC)]
        h_ready = [sem(f"h_ready{c}") for c in range(KC)]
        pair_hi_ready = sem("pair_hi_ready")
        pair_lo_ready = sem("pair_lo_ready")
        yT_ready = sem("yT_ready")
        y_ps = sem("y_ps")
        y_ready = sem("y_ready")
        out_done = [sem("out_done0"), sem("out_done1")]

        def group(base, u, lag, count=NG):
            g = base + (u - lag)
            if isinstance(g, int) and not 0 <= g < count:
                return None
            return g

        def later(g, n):
            return not isinstance(g, int) or g >= n

        def spread(g, slot):
            return (g - slot) * (8 * NB) + 16 * NB

        def pipeline(eng, body, last):
            for i in range(FIRST_LOOPED):
                body(i - i % UNROLL, i % UNROLL)
            with eng.Fori(FIRST_LOOPED // UNROLL, NG // UNROLL) as q:
                for u in range(UNROLL):
                    body(q * UNROLL, u)
            for i in range(NG, last + 1):
                body(i - i % UNROLL, i % UNROLL)

        def draining(base, u):
            return isinstance(base, int) and base + u >= NG + LAG_QKT

        def filling(base, u):
            return isinstance(base, int) and base + u <= LAG_QK

        def norm_item(base, u):
            n = group(base, u, LAG_X, NG + LAG_QK)
            return None if isinstance(n, int) and n < LAG_QK else n

        def norm_columns(n):
            return 0, (NS - 1 if isinstance(n, int) and not FIRST_NORMED <= n < NG else NS)

        gru_banks = ((p_qkT, p_xT, p_qk[0], p_qk[1]), (p_vx2, p_s, p_o, p_w))

        def gru_bank(pair_slot, chunk, part):
            return gru_banks[pair_slot][2 * chunk + part]

        def pair_index(base, n):
            return (base // 4) * 2 + n if isinstance(base, int) else turn[0] * 2 + n

        def has_pair(base, n):
            return not isinstance(base, int) or base // 2 + n < T // 2

        def x2T_pair(u):
            return x2T[:, :].rearrange("p (c u n) -> p c u n", c=KC, n=2 * B)[:, :, u, :]

        turn = [0]

        def gru_steps(eng, body):
            for s in range(4):
                body(0, s)
            with eng.Fori(1, T // 4 - 1) as q:
                turn[0] = q
                for s in range(4):
                    body(q * 4, s)
            for s in range(4):
                body(T - 4, s)

        R_COL, Z_COL, IN_COL, HN_COL, SPARE_COL = 0, 2 * B, 0, 2 * B, 3 * B

        block = ctx.enter_context(nc.Block())

        @block.sync
        def _(sp):
            x_groups = x.rearrange("(g b) t d -> (b t) g d", b=GB)

            def load_x(i):
                n = NG // len(x_loaded)
                sp.dma_start(x_in[:, n * i:n * i + n, :], x_groups[:, n * i:n * i + n, :]).then_inc(x_loaded[i], 16)

            sp.dma_start(cond_sb[:, :], cond).then_inc(cond_loaded, 16)
            load_x(0)
            for row, vector in ((12, b_emb), (16, g_norm), (0, b_ih), (6, b_hh)):
                n = vector.shape[0] // P
                sp.dma_start(vec_rows[row:row + n, :], vector.rearrange("(n p) -> n p", p=P)).then_inc(vec_loaded, 16)
            for row, gain in ((18, g_q), (19, g_k)):
                sp.dma_start(vec_rows[row:row + 1, :].rearrange("o (h d) -> o h d", d=DH),
                             gain.unsqueeze(0).unsqueeze(0).broadcast_to([1, HC, DH])).then_inc(vec_loaded, 16)
            load_x(1)
            sp.dma_start(stage_wo[:, :, :], w_out.rearrange("(c p) n -> p c n", p=P)).then_inc(wo_loaded, 16)
            load_x(2)
            load_x(3)
            sp.dma_start(w_hh_sb[:, :, :], w_hh.rearrange("(c p) n -> p c n", p=P)).then_inc(hh_loaded, 16)
            for i in range(4, len(x_loaded)):
                load_x(i)
            sp.wait_ge(wqkv_ready, 1)
            sp.dma_start(stage_w[:, :, :], w_ih.rearrange("(c p) n -> p c n", p=P)).then_inc(ih_loaded, 16)

            sp.wait_ge(k_diag_clear, 1)

            def body(base, u):
                g = group(base, u, LAG_KEYS)
                if g is not None:
                    slot = (u - LAG_KEYS) % 2
                    sp.wait_ge(k_masked_ready, g + 1)
                    for n in range(NB):
                        rows = slice(PB * n, PB * n + PB)
                        sp.dma_start(k_diag[rows, slot, n, :, :, :].rearrange("p r j k -> p (r j k)"),
                                     k_masked[rows, slot, :, :].rearrange("p r f -> p (r f)"))\
                          .then_inc(k_diag_ready[slot], 16)

            pipeline(sp, body, NG - 1 + LAG_KEYS)

            with sp.Fori(0, T // 4) as q:
                for slot in range(2):
                    sp.wait_ge(y_ready, q * 4 + 2 * slot + 2)
                    sp.wait_ge(x2T_ready, NG)
                    sp.dma_start(out[:, :, :].rearrange("b (u e) d -> b u (e d)", e=2)[:, q * 2 + slot, :],
                                 y_out[:, slot, :, :].rearrange("p e d -> p (e d)")).then_inc(out_done[slot], 16)
            for slot in range(2):
                sp.wait_ge(out_done[slot], 16 * (T // 4))

        @block.gpsimd
        def _(pool):
            pool.memset(ident[:, :], 0.0).then_inc(ident_zero, 1)
            pool.wait_ge(ident_zero, 1)
            pool.affine_select(out=ident[:, :], in_=ident[:, :], compare_op=ALU.not_equal, fill=1.0, base=0,
                               pattern=[[-1, P]], channel_multiplier=1).then_inc(ident_ready, 1)

            def body(base, u):
                k = group(base, u, LAG_KEYS)
                if k is not None:
                    slot = (u - LAG_KEYS) % 2
                    pool.wait_ge(qkT_ready, k + 1)
                    if later(k, 2):
                        pool.wait_ge(k_diag_ready[slot], spread(k - 2, slot))
                    if isinstance(k, int) and k == 0:
                        pool.wait_ge(vec_ready, 3)
                    pool.tensor_tensor(k_masked[:, slot, :, :],
                                       qkT[:, slot, D:2 * D].unsqueeze(1).broadcast_to([P, 2, D]),
                                       gqk_parity[:, :].unsqueeze(2).broadcast_to([P, 2, D]),
                                       ALU.mult).then_inc(k_masked_ready, 1)
                g = group(base, u, LAG_MOD)
                if g is not None:
                    slot = (u - LAG_MOD) % 2
                    shift = mod_shift[:, :, g, :].unsqueeze(3).broadcast_to([P, KC, GB, T])
                    pool.wait_ge(xmod_ready, g + 1)
                    if isinstance(g, int) and g == 0:
                        pool.wait_ge(mod_ready, 1)
                    if later(g, 2):
                        pool.wait_ge(xn_lo_ready, g - 1)
                    pool.tensor_tensor(xn[:, slot, :].rearrange("p (c b t) -> p c b t", c=KC, b=GB),
                                       xmod[:, slot, :].rearrange("p (c b t) -> p c b t", c=KC, b=GB),
                                       shift, ALU.add).then_inc(xn_ready, 1)
                o = group(base, u, LAG_OUT)
                if o is not None:
                    slot = (u - LAG_OUT) % 2
                    pool.wait_ge(oT_hi_ready, o + 1)
                    if later(o, 2):
                        pool.wait_ge(w_ps, o - 1)
                    pool.tensor_tensor(oT_lo[:, slot, :].rearrange("p (c b t) -> p b c t", c=KC, b=GB),
                                       oT[:, slot, :].rearrange("p (b c t) -> p b c t", c=KC, b=GB),
                                       oT_hi[:, slot, :].bitcast(F32).rearrange("p (c b t) -> p b c t", c=KC, b=GB),
                                       ALU.subtract).then_inc(oT_lo_ready, 1)
                if g is not None:
                    slot = (u - LAG_MOD) % 2
                    pool.wait_ge(xn_hi_ready, g + 1)
                    if later(g, 2):
                        pool.wait_ge(v_ps, g - 1)
                    pool.tensor_tensor(xn_lo[:, slot, :], xn[:, slot, :], xn_hi[:, slot, :].bitcast(F32),
                                       ALU.subtract).then_inc(xn_lo_ready, 1)
                n = norm_item(base, u)
                if n is not None:
                    nslot = u % 2
                    lo, hi = norm_columns(n)
                    y0, a, b = rs0[:, nslot, lo:hi], newton_a[:, nslot, lo:hi], newton_b[:, nslot, lo:hi]
                    pool.wait_ge(rs0_ready, n + 1)
                    pool.tensor_tensor(a, y0, y0, ALU.mult).then_inc(newton_step, 1)
                    pool.wait_ge(newton_step, 3 * n + 1)
                    pool.tensor_tensor(b, a, ms4[:, nslot, lo:hi], ALU.mult).then_inc(newton_step, 1)
                    pool.wait_ge(newton_step, 3 * n + 2)
                    pool.tensor_tensor(a, threes[:, lo:hi], b, ALU.subtract).then_inc(newton_step, 1)
                    pool.wait_ge(newton_step, 3 * n + 3)
                    pool.tensor_tensor(rs[:, nslot, lo:hi], a, y0, ALU.mult).then_inc(rs_ready, 1)

            pool.memset(threes[:, :], 3.0).then_inc(threes_ready, 1)
            pool.memset(v_diag[:, :, :, :, :], 0.0).then_inc(v_diag_clear, 1)
            pool.wait_ge(v_diag_clear, 1)
            for b in range(GB):
                last = pool.memset(v_diag[T * b:T * b + T, :, b, :, DH:VW], 1.0)
            last.then_inc(ones_ready, 1)
            pool.wait_ge(threes_ready, 1)
            pool.wait_ge(ones_ready, 1)
            first = [norm_first[:, i, :] for i in range(7)]
            pool.wait_ge(rs0_ready, LAG_QK)
            pool.tensor_tensor(first[4], first[3], first[3], ALU.mult).then_inc(newton_step, LAG_QK)
            pool.wait_ge(newton_step, LAG_QK)
            pool.tensor_tensor(first[5], first[4], first[1], ALU.mult).then_inc(newton_step, LAG_QK)
            pool.wait_ge(newton_step, 2 * LAG_QK)
            pool.tensor_tensor(first[4], threes[:, 0:FIRST_NORMED], first[5], ALU.subtract).then_inc(newton_step, LAG_QK)
            pool.wait_ge(newton_step, 3 * LAG_QK)
            pool.tensor_tensor(first[6], first[4], first[3], ALU.mult).then_inc(rs_ready, LAG_QK)
            pipeline(pool, body, NG - 1 + LAG_OUT)
            pool.wait_ge(x2T_ready, NG)

            def split_pair(u, slot):
                pool.wait_ge(pair_hi_ready, u + 1)
                pool.tensor_tensor(pair_lo[:, slot, :, :], x2T_pair(u), pair_hi[:, slot, :, :].bitcast(F32),
                                   ALU.subtract).then_inc(pair_lo_ready, 1)

            pool.wait_ge(pair_lo_ready, 1)
            split_pair(1, 1)

            def step(base, s):
                t = base + s
                for c in range(KC):
                    pool.wait_ge(z_ready[c], t + 1)
                    pool.tensor_tensor(zh[:, c, :], z_g[:, c, :], h[:, (s + 1) % 2, c, :],
                                       ALU.mult).then_inc(zh_ready[c], 1)
                pool.wait_ge(h_ready[0], t + 1)
                pool.wait_ge(h_ready[1], t + 1)
                if later(t, 2):
                    pool.wait_ge(y_ps, t - 1)
                pool.tensor_tensor(yT[:, s % 2, :, :], h[:, s % 2, :, :],
                                   x2T[:, :].rearrange("p (c t b) -> p c t b", c=KC, b=B)[:, :, t, :],
                                   ALU.add).then_inc(yT_ready, 1)
                if s % 2 == 0 and has_pair(base, s // 2 + 2):
                    split_pair(pair_index(base, s // 2 + 2), s // 2)

            gru_steps(pool, step)

        @block.scalar
        def _(act):
            act.dma_start(w_emb_sb[:, :, :], w_emb.rearrange("(c p) n -> p c n", p=P)).then_inc(emb_loaded, 16)
            act.dma_start(stage_w[:, :, :], w_qkv.rearrange("(c p) n -> p c n", p=P)).then_inc(qkv_loaded, 16)
            act.preload_act_table_set("natural_log_exp_and_others")
            act.wait_ge(condT_ps, 1)
            act.copy(h[:, 1, :, :], p_w[:, 0:KC * B].rearrange("p (c b) -> p c b", c=KC)).then_inc(condT_ready, 1)

            act.wait_ge(x_loaded[0], 16)
            for n in range(FIRST_NORMED):
                if n >= 1:
                    act.wait_ge(ssx_ready, n)
                act.activation(square_x[:, :], x_in[:, n, :], ACT.Square, scale=(DH / D) ** 0.5,
                               accum_out=norm_first[:, 0, n:n + 1]).then_inc(ssx_ready, 1)
            act.wait_ge(ms4_ready, LAG_QK)
            act.activation(norm_first[:, 2, :], norm_first[:, 1, :], ACT.Ln).then_inc(ln_ready, LAG_QK)
            act.wait_ge(ln_ready, LAG_QK)
            act.activation(norm_first[:, 3, :], norm_first[:, 2, :], ACT.Exp, scale=-0.5).then_inc(rs0_ready, LAG_QK)

            def vectors_and_projection_weights():
                act.wait_ge(vec_ps, 1)
                act.copy(vec_cols[:, :], p_o[:, 0:20]).then_inc(vec_cols_ready, 1)
                act.wait_ge(qkv_loaded, 16)
                act.copy(wqkv_hi[:, :, :], stage_w[:, :, :]).then_inc(wqkv_hi_ready, 1)

            def result(d):
                if d is not None:
                    act.copy(x2T[:, :].rearrange("p (c t g b) -> p c t g b", c=KC, t=T, b=GB)[:, :, :, d, :],
                             p_x2T.rearrange("p (c b t) -> p c t b", c=KC, b=GB)).then_inc(x2T_ready, 1)

            def input_high_part(m, slot):
                if m is not None:
                    act.wait_ge(xn_ready, m + 1)
                    if later(m, 2):
                        act.wait_ge(v_ps, m - 1)
                    act.copy(xn_hi[:, slot, :], xn[:, slot, :]).then_inc(xn_hi_ready, 1)

            def body(base, u):
                m = group(base, u, LAG_MOD)
                n = group(base, u, LAG_X)
                nslot = u % 2
                if isinstance(n, int) and n < FIRST_NORMED:
                    n = None
                if n is not None:
                    if isinstance(n, int):
                        if n % 4 == 0:
                            act.wait_ge(x_loaded[n // 4], 16)
                        if n == FIRST_LOOPED - 1:
                            for loaded in x_loaded[FIRST_LOOPED // 4:]:
                                act.wait_ge(loaded, 16)
                    if later(n, 1):
                        act.wait_ge(ssx_ready, n)
                g = group(base, u, LAG_PV)
                if g is not None:
                    slot = (u - LAG_PV) % 2
                    act.wait_ge(logits_ready, g + 1)
                    if later(g, 2):
                        act.wait_ge(probsT_ready, g - 1)
                    act.activation(probs[:, slot, :], logits[:, slot, :], ACT.Exp).then_inc(probs_ready, 1)
                if draining(base, u) and draining(base, u - 1):
                    act.wait_ge(x2T_ps, base + u - LAG_X2T)
                    result(base + u - LAG_X2T - 1)
                if isinstance(base, int) and base + u == NG + LAG_QKT:
                    act.wait_ge(ih_loaded, 16)
                    act.copy(wih_hi[:, :, :], stage_w[:, :, :]).then_inc(wih_hi_ready, 1)
                if n is not None:
                    act.activation(square_x[:, :], x_in[:, n, :], ACT.Square, scale=(DH / D) ** 0.5,
                                   accum_out=ss[:, nslot, NS - 1:NS]).then_inc(ssx_ready, 1)
                if filling(base, u):
                    input_high_part(m, (u - LAG_MOD) % 2)
                g = group(base, u, LAG_QK)
                if g is not None:
                    act.wait_ge(qk_ps, g + 1)
                    act.activation(square_qk[:, :], p_qk[(u - LAG_QK) % 2][:, :], ACT.Square).then_inc(sq_ready, 1)
                g = group(base, u, LAG_OUT)
                if g is not None:
                    slot = (u - LAG_OUT) % 2
                    act.wait_ge(oT_ready, g + 1)
                    if later(g, 2):
                        act.wait_ge(w_ps, g - 1)
                    act.copy(oT_hi[:, slot, :].rearrange("p (c b t) -> p b c t", c=KC, b=GB),
                             oT[:, slot, :].rearrange("p (b c t) -> p b c t", c=KC, b=GB))\
                       .then_inc(oT_hi_ready, 1)

                def values(sequences):
                    for b in sequences:
                        rows = slice(T * b, T * b + T)
                        last = act.copy(v_diag[rows, (u - LAG_V) % 4, b, :, 0:DH],
                                        p_v[rows, :].rearrange("p (h d) -> p h d", h=HEADS))
                    return last

                v = group(base, u, LAG_V)
                if v is not None:
                    act.wait_ge(v_ps, v + 1)
                    if later(v, 4):
                        act.wait_ge(o_ps, v - 3)
                    if isinstance(v, int) and v == 0:
                        act.wait_ge(ones_ready, 1)
                d = group(base, u, LAG_X2T)
                if d is not None and not draining(base, u):
                    act.wait_ge(x2T_ps, d + 1)
                if v is not None:
                    values(range(0, 2))
                if not draining(base, u):
                    result(d)
                x_hat = group(base, u, LAG_HAT)
                if x_hat is not None:
                    first = isinstance(x_hat, int) and x_hat < FIRST_NORMED
                    act.wait_ge(rs_ready, LAG_QK if first else x_hat + 1)
                    if later(x_hat, 2):
                        act.wait_ge(xT_ps, x_hat - 1)
                if not filling(base, u):
                    input_high_part(m, (u - LAG_MOD) % 2)
                if x_hat is not None:
                    slot = (u - LAG_HAT) % 2
                    act.activation(xhat[:, slot, :], x_in[:, x_hat, :], ACT.Copy,
                                   scale=norm_first[:, 6, x_hat:x_hat + 1] if first else rs[:, slot, NS - 1:NS])\
                       .then_inc(xhat_ready, 1)
                n = norm_item(base, u)
                if n is not None:
                    lo, hi = norm_columns(n)
                    act.wait_ge(ms4_ready, n + 1)
                    act.activation(ln_ms[:, nslot, lo:hi], ms4[:, nslot, lo:hi], ACT.Ln).then_inc(ln_ready, 1)
                    act.wait_ge(ln_ready, n + 1)
                    act.activation(rs0[:, nslot, lo:hi], ln_ms[:, nslot, lo:hi], ACT.Exp,
                                   scale=-0.5).then_inc(rs0_ready, 1)
                if v is not None:
                    values(range(2, GB)).then_inc(v_ready, 1)
                g = group(base, u, LAG_QKT)
                if g is not None:
                    slot = (u - LAG_QKT) % 2
                    act.wait_ge(qkT_ps, g + 1)
                    if later(g, 2):
                        act.wait_ge(k_masked_ready, g - 1)
                    act.copy(qkT[:, slot, :], p_qkT[:, :]).then_inc(qkT_ready, 1)
                if isinstance(base, int) and base + u == 0:
                    vectors_and_projection_weights()

            pipeline(act, body, NG + LAG_X2T)

            act.wait_ge(x2T_ready, NG)

            def split_pair(u, slot):
                act.copy(pair_hi[:, slot, :, :], x2T_pair(u)).then_inc(pair_hi_ready, 1)

            split_pair(0, 0)
            act.preload_act_table(ACT.Sigmoid)
            split_pair(1, 1)
            act.wait_ge(gru_bias_ready, 1)

            def step(base, s):
                t = base + s
                pair_slot, e = s // 2, s % 2
                for c in range(KC):
                    rz, xnh = gru_bank(pair_slot, c, 0), gru_bank(pair_slot, c, 1)
                    r_in = rz[:, R_COL + e * B:R_COL + e * B + B]
                    z_in = rz[:, Z_COL + e * B:Z_COL + e * B + B]
                    act.wait_ge(gates_ps[c], t + 1)
                    act.activation(r_g[:, c, :], r_in, ACT.Sigmoid, bias=bsum[:, c:c + 1]).then_inc(r_ready[c], 1)
                    act.activation(z_g[:, c, :], z_in, ACT.Sigmoid,
                                   bias=bsum[:, KC + c:KC + c + 1]).then_inc(z_ready[c], 1)
                    act.activation(omz[:, c, :], z_in, ACT.Sigmoid, bias=bneg[:, KC + c:KC + c + 1],
                                   scale=-1.0).then_inc(omz_ready[c], 1)
                    act.wait_ge(npre_ready[c], t + 1)
                    act.activation(n_g[:, c, :], npre[:, c, :], ACT.Tanh,
                                   bias=bih[:, 2 * KC + c:2 * KC + c + 1]).then_inc(n_ready[c], 1)
                if e == 0 and has_pair(base, s // 2 + 2):
                    split_pair(pair_index(base, s // 2 + 2), s // 2)

            gru_steps(act, step)

        @block.vector
        def _(dve):
            dve.memset(operands[:, 0:KD], 0.0).then_inc(k_diag_clear, 1)
            dve.wait_ge(ident_ready, 1)
            dve.tensor_reduce(head_rows[:, :], ident[:, :].rearrange("p (h d) -> p h d", d=DH),
                              AX_X, ALU.add).then_inc(parity_step, 1)
            dve.wait_ge(parity_step, 1)
            dve.tensor_reduce(parity[:, :], head_rows[:, :].rearrange("p (n r) -> p r n", r=2),
                              AX_X, ALU.add).then_inc(parity_step, 1)
            dve.wait_ge(ssx_ready, FIRST_NORMED)
            dve.tensor_scalar(norm_first[:, 1, :], norm_first[:, 0, :], 4.0 / DH, 4.0 * RMS_EPS,
                              ALU.mult, ALU.add).then_inc(ms4_ready, LAG_QK)

            def modulation():
                dve.wait_ge(vec_cols_ready, 1)
                dve.scalar_tensor_tensor(out=gqk[:, :], in0=gq_col, scalar=DH ** -0.5, in1=gk_col,
                                         op0=ALU.mult, op1=ALU.mult).then_inc(vec_ready, 1)
                dve.wait_ge(parity_step, 2)
                dve.wait_ge(vec_ready, 1)
                dve.tensor_scalar(gqk_parity[:, :], parity[:, :], gqk[:, 0:1], None, ALU.mult).then_inc(vec_ready, 1)
                dve.tensor_scalar(bemb1[:, :], bemb[:, 0:KC], 1.0, None, ALU.add).then_inc(vec_ready, 1)
                dve.wait_ge(emb_ps, 1)
                dve.wait_ge(vec_ready, 3)
                for c in range(KC):
                    dve.tensor_scalar(mod_scale[:, c, :, :].rearrange("p g b -> p (g b)"), p_s[:, c * B:c * B + B],
                                      bemb1[:, c:c + 1], gnorm[:, c:c + 1], ALU.add, ALU.mult)
                for c in range(KC):
                    last = dve.tensor_scalar(mod_shift[:, c, :, :].rearrange("p g b -> p (g b)"),
                                             p_s[:, (KC + c) * B:(KC + c) * B + B], bemb[:, KC + c:KC + c + 1], None,
                                             ALU.add)
                last.then_inc(mod_ready, 1)

            def projection_weights():
                dve.wait_ge(wqkv_hi_ready, 1)
                dve.tensor_tensor(wqkv_lo[:, :, :], stage_w[:, :, :], wqkv_hi[:, :, :].bitcast(F32),
                                  ALU.subtract).then_inc(wqkv_ready, 1)

            def output_weights():
                dve.wait_ge(wo_loaded, 16)
                dve.wait_ge(ident_ready, 1)
                for c in range(KC):
                    last = dve.tensor_tensor(stage_wo[:, c, c * P:c * P + P], stage_wo[:, c, c * P:c * P + P],
                                             ident[:, :], ALU.add)
                last.then_inc(wo_sum, 1)
                dve.wait_ge(wo_sum, 1)
                dve.tensor_copy(wo_hi[:, :, :], stage_wo[:, :, :]).then_inc(wo_hi_ready, 1)
                dve.wait_ge(wo_hi_ready, 1)
                dve.tensor_tensor(wo_lo[:, :, :], stage_wo[:, :, :], wo_hi[:, :, :].bitcast(F32),
                                  ALU.subtract).then_inc(wo_ready, 1)

            def gru_biases():
                dve.tensor_tensor(bsum[:, :], bih[:, 0:2 * KC], bhh[:, 0:2 * KC], ALU.add).then_inc(gru_bias, 1)
                dve.wait_ge(gru_bias, 1)
                dve.tensor_scalar(bneg[:, :], bsum[:, :], -1.0, None, ALU.mult).then_inc(gru_bias_ready, 1)

            def residual(o, slot):
                if o is not None:
                    dve.wait_ge(w_ps, o + 1)
                    if later(o, 2):
                        dve.wait_ge(x2T_ps, o - 1)
                    dve.tensor_tensor(x2[:, slot, :], p_w[:, 0:D], x_in[:, o, :], ALU.add).then_inc(x2_ready, 1)

            def body(base, u):
                o = group(base, u, LAG_OUT)
                if o is not None:
                    slot = (u - LAG_OUT) % 2
                    o_heads = p_o[:, 0:GB * HEADS // 4 * VW].rearrange("p (n f) -> p n f", f=VW)
                    dve.wait_ge(o_ps, o + 1)
                    dve.reciprocal(inv_sum[:, slot, :], o_heads[:, :, DH]).then_inc(inv_ready, 1)
                if not draining(base, u):
                    residual(group(base, u, LAG_OUT + 1), (u - LAG_OUT - 1) % 2)
                if o is not None:
                    dve.wait_ge(inv_ready, o + 1)
                    dve.tensor_tensor(o_sb[:, slot, :].rearrange("p (n d) -> p n d", d=DH), o_heads[:, :, 0:DH],
                                      inv_sum[:, slot, :].unsqueeze(2).broadcast_to([P, HEADS, DH]),
                                      ALU.mult).then_inc(o_ready, 1)
                g = group(base, u, LAG_PV)
                if g is not None:
                    slot = (u - LAG_PV) % 2
                    dve.wait_ge(probs_ready, g + 1)
                    if later(g, 2):
                        dve.wait_ge(o_ps, g - 1)
                    dve.transpose(probsT[:, slot, :, :].rearrange("p h q -> p (h q)"), probs[:, slot, :])\
                       .then_inc(probsT_ready, 1)
                if o is not None:
                    slot = (u - LAG_OUT) % 2
                    dve.wait_ge(o_ready, o + 1)
                    if later(o, 2):
                        dve.wait_ge(oT_lo_ready, o - 1)
                    dve.transpose(oT[:, slot, :], o_sb[:, slot, :]).then_inc(oT_ready, 1)
                if draining(base, u):
                    residual(group(base, u, LAG_OUT + 1), (u - LAG_OUT - 1) % 2)
                if draining(base, u) and base + u - NG - LAG_QKT < KC:
                    c = base + u - NG - LAG_QKT
                    dve.wait_ge(wih_hi_ready, 1)
                    dve.tensor_tensor(wih_lo[:, c, :], stage_w[:, c, :], wih_hi[:, c, :].bitcast(F32),
                                      ALU.subtract).then_inc(wih_ready, 1)
                g = group(base, u, LAG_MOD)
                if g is not None:
                    slot = (u - LAG_MOD) % 2
                    dve.wait_ge(xT_ps, g + 1)
                    if isinstance(g, int) and g == 0:
                        dve.wait_ge(mod_ready, 1)
                    if later(g, 2):
                        dve.wait_ge(xn_ready, g - 1)
                    dve.tensor_tensor(xmod[:, slot, :].rearrange("p (c b t) -> p c b t", c=KC, b=GB),
                                      p_xT[:, 0:D].rearrange("p (c b t) -> p c b t", c=KC, b=GB),
                                      mod_scale[:, :, g, :].unsqueeze(3).broadcast_to([P, KC, GB, T]),
                                      ALU.mult).then_inc(xmod_ready, 1)
                g = group(base, u, LAG_QKT)
                if g is not None:
                    slot = (u - LAG_QKT) % 2
                    dve.wait_ge(rs_ready, g + LAG_QK + 1)
                    if later(g, 2):
                        dve.wait_ge(qkT_ps, g - 1)
                    dve.tensor_tensor(qkn[:, slot, :].rearrange("p (h d) -> p h d", d=DH),
                                      p_qk[slot][:, :].rearrange("p (h d) -> p h d", d=DH),
                                      rs[:, (u - 1) % 2, 0:2 * HEADS].unsqueeze(2).broadcast_to([P, 2 * HEADS, DH]),
                                      ALU.mult).then_inc(qkn_ready, 1)
                g = group(base, u, LAG_QK)
                nslot = u % 2
                if g is not None:
                    dve.wait_ge(sq_ready, g + 1)
                    dve.tensor_reduce(ss[:, nslot, 0:2 * HEADS],
                                      square_qk[:, :].rearrange("p (h d) -> p h d", d=DH),
                                      AX_X, ALU.add).then_inc(ssqk_ready, 1)
                n = norm_item(base, u)
                if n is not None:
                    lo, hi = norm_columns(n)
                    dve.wait_ge(ssqk_ready, g + 1)
                    if hi == NS:
                        dve.wait_ge(ssx_ready, n + 1)
                    dve.tensor_scalar(ms4[:, nslot, lo:hi], ss[:, nslot, lo:hi], 4.0 / DH, 4.0 * RMS_EPS,
                                      ALU.mult, ALU.add).then_inc(ms4_ready, 1)
                g = group(base, u, LAG_S)
                s_heads = p_s[:, :].rearrange("p (h k) -> p h k", h=HEADS)
                if g is not None:
                    slot = (u - LAG_S) % 2
                    dve.wait_ge(s_ps, g + 1)
                    dve.tensor_reduce(row_max[:, slot, :], s_heads, AX_X, ALU.max).then_inc(max_ready, 1)
                if g is not None:
                    slot = (u - LAG_S) % 2
                    dve.wait_ge(max_ready, g + 1)
                    if later(g, 2):
                        dve.wait_ge(probs_ready, g - 1)
                    dve.tensor_tensor(logits[:, slot, :].rearrange("p (h k) -> p h k", h=HEADS), s_heads,
                                      row_max[:, slot, :].unsqueeze(2).broadcast_to([P, HEADS, T]),
                                      ALU.subtract).then_inc(logits_ready, 1)
                if isinstance(base, int) and base + u == LAG_X:
                    modulation()
                if isinstance(base, int) and base + u == LAG_MOD:
                    projection_weights()
                if isinstance(base, int) and base + u == LAG_V:
                    gru_biases()
                    output_weights()

            pipeline(dve, body, NG + LAG_OUT)
            dve.wait_ge(pair_hi_ready, 1)
            dve.tensor_tensor(pair_lo[:, 0, :, :], x2T_pair(0), pair_hi[:, 0, :, :].bitcast(F32),
                              ALU.subtract).then_inc(pair_lo_ready, 1)

            def store_step(t, s, pair_slot):
                dve.wait_ge(y_ps, t + 1)
                if s % 2 == 0 and later(t, 4):
                    dve.wait_ge(out_done[s // 2], (t - s) * 4)
                for c in range(KC):
                    last = dve.tensor_copy(y_out[:, s // 2, s % 2, c * P:c * P + P],
                                           gru_bank(pair_slot, c, 1)[:, SPARE_COL:SPARE_COL + P])
                last.then_inc(y_ready, 1)

            def step(base, s):
                t = base + s
                pair_slot, e = s // 2, s % 2
                for c in range(KC):
                    xnh = gru_bank(pair_slot, c, 1)
                    dve.wait_ge(r_ready[c], t + 1)
                    dve.scalar_tensor_tensor(out=rh[:, c, :], in0=xnh[:, HN_COL:HN_COL + B],
                                             scalar=bhh[:, 2 * KC + c:2 * KC + c + 1], in1=r_g[:, c, :],
                                             op0=ALU.add, op1=ALU.mult).then_inc(rh_ready[c], 1)
                    dve.wait_ge(rh_ready[c], t + 1)
                    dve.tensor_tensor(npre[:, c, :], xnh[:, IN_COL + e * B:IN_COL + e * B + B], rh[:, c, :],
                                      ALU.add).then_inc(npre_ready[c], 1)
                    if c == 0 and later(t, 1):
                        store_step(t - 1, (s - 1) % 4, 1 - pair_slot)
                    dve.wait_ge(n_ready[c], t + 1)
                    dve.tensor_tensor(zn[:, c, :], omz[:, c, :], n_g[:, c, :], ALU.mult).then_inc(zn_ready[c], 1)
                    dve.wait_ge(zn_ready[c], t + 1)
                    dve.wait_ge(zh_ready[c], t + 1)
                    if later(t, 2):
                        dve.wait_ge(yT_ready, t - 1)
                    dve.tensor_tensor(h[:, s % 2, c, :], zn[:, c, :], zh[:, c, :], ALU.add).then_inc(h_ready[c], 1)

            gru_steps(dve, step)
            store_step(T - 1, 3, 0)

        @block.tensor
        def _(pe):
            def products(dst, hi, lo, whi, wlo, start=True):
                terms = [(a[c], w[c]) for c in range(KC) for a, w in ((hi, whi), (hi, wlo), (lo, whi))]
                for i, (a, w) in enumerate(terms):
                    last = pe.matmul(dst, a, w, start=start and i == 0, stop=i == len(terms) - 1,
                                     skip_group_check=True)
                return last

            pe.wait_ge(ident_ready, 1)
            pe.wait_ge(cond_loaded, 16)
            for c in range(KC):
                last = pe.transpose(p_w[:, c * B:c * B + B], cond_sb[:, c * P:c * P + P], ident[:, :])
            last.then_inc(condT_ps, 1)
            pe.wait_ge(condT_ready, 1)
            pe.wait_ge(emb_loaded, 16)
            for m in range(2 * KC):
                for c in range(KC):
                    last = pe.matmul(p_s[:, m * B:m * B + B], w_emb_sb[:, c, m * P:m * P + P], h[:, 1, c, :],
                                     start=c == 0, stop=c == KC - 1)
            last.then_inc(emb_ps, 1)
            pe.wait_ge(vec_loaded, 16 * 6)
            pe.transpose(p_o[:, 0:20], vec_rows[:, :], ident[0:20, 0:20]).then_inc(vec_ps, 1)

            def projection_input(u, lag):
                slot = (u - lag) % 2
                return ([xn_hi[:, slot, c * P:c * P + P] for c in range(KC)],
                        [xn_lo[:, slot, c * P:c * P + P] for c in range(KC)])

            def gate(weights, name, c):
                col = "rzn".index(name) * D + c * P
                return [weights[:, k, col:col + P] for k in range(KC)]

            def input_gates(slot, c, part):
                xhi = [pair_hi[:, slot, k, :] for k in range(KC)]
                xlo = [pair_lo[:, slot, k, :] for k in range(KC)]
                for name, col in ((("r", R_COL), ("z", Z_COL)), (("n", IN_COL),))[part]:
                    whi, wlo = gate(wih_hi, name, c), gate(wih_lo, name, c)
                    dst = gru_bank(slot, c, part)[:, col:col + 2 * B]
                    products(dst, whi, wlo, xhi, xlo, start=name != "z")

            def state_gates(s, c, k, opens=False):
                slot, e = s // 2, s % 2
                rz, xnh = gru_bank(slot, c, 0), gru_bank(slot, c, 1)
                moving = h[:, (s + 1) % 2, k, :]
                for name, dst in (("z", rz[:, Z_COL + e * B:Z_COL + e * B + B]), ("n", xnh[:, HN_COL:HN_COL + B]),
                                  ("r", rz[:, R_COL + e * B:R_COL + e * B + B])):
                    last = pe.matmul(dst, gate(w_hh_sb, name, c)[k], moving,
                                     start=k == 0 and (name == "n" or opens and name == "z"), stop=k == KC - 1,
                                     skip_group_check=True)
                return last

            def first_input_gates(c):
                gates = [(name, gru_bank(0, c, part)[:, col:col + 2 * B])
                         for name, part, col in (("r", 0, R_COL), ("z", 0, Z_COL), ("n", 1, IN_COL))]
                pe.wait_ge(pair_hi_ready, 1)
                for name, dst in gates:
                    for weights in (wih_hi, wih_lo):
                        for k in range(KC):
                            pe.matmul(dst, gate(weights, name, c)[k], pair_hi[:, 0, k, :], start=False, stop=False,
                                      skip_group_check=True)
                pe.wait_ge(pair_lo_ready, 1)
                for name, dst in gates:
                    for k in range(KC):
                        last = pe.matmul(dst, gate(wih_hi, name, c)[k], pair_lo[:, 0, k, :], start=False,
                                         stop=k == KC - 1, skip_group_check=True)
                return last

            def query_key_products(base, u):
                g = group(base, u, LAG_QK)
                if g is not None:
                    pe.wait_ge(xn_lo_ready, g + 1)
                    if isinstance(g, int) and g == 0:
                        pe.wait_ge(wqkv_ready, 1)
                    if later(g, 2):
                        pe.wait_ge(qkn_ready, g - 1)
                    hi, lo = projection_input(u, LAG_QK)
                    products(p_qk[(u - LAG_QK) % 2][:, :], hi, lo, [wqkv_hi[:, c, 0:2 * D] for c in range(KC)],
                             [wqkv_lo[:, c, 0:2 * D] for c in range(KC)]).then_inc(qk_ps, 1)

            def input_transposes(base, u):
                g = group(base, u, LAG_MOD)
                if g is not None:
                    pe.wait_ge(xhat_ready, g + 1)
                    if later(g, 1):
                        pe.wait_ge(xmod_ready, g)
                    for c in range(KC):
                        last = pe.transpose(p_xT[:, c * P:c * P + P], xhat[:, (u - LAG_MOD) % 2, c * P:c * P + P],
                                            ident[:, :])
                    last.then_inc(xT_ps, 1)

            FIRST_GATES = (((0, 0),), ((0, 1),), (), ((1, 0),), ((1, 1),))

            def result_transposes(base, u):
                d = group(base, u, LAG_X2T)
                if d is not None:
                    if later(d, 1):
                        pe.wait_ge(x2T_ready, d)
                    pe.wait_ge(x2_ready, d + 1)
                    for c in range(KC):
                        last = pe.transpose(p_x2T[:, c * P:c * P + P], x2[:, (u - LAG_X2T) % 2, c * P:c * P + P],
                                            ident[:, :])
                    last.then_inc(x2T_ps, 1)

            def output_projection(base, u):
                g = group(base, u, LAG_OUT)
                if g is not None:
                    slot = (u - LAG_OUT) % 2
                    pe.wait_ge(oT_lo_ready, g + 1)
                    if isinstance(g, int) and g == 0:
                        pe.wait_ge(wo_ready, 1)
                    if later(g, 1):
                        pe.wait_ge(x2_ready, g)
                    products(p_w[:, 0:D], [oT_hi[:, slot, c * P:c * P + P] for c in range(KC)],
                             [oT_lo[:, slot, c * P:c * P + P] for c in range(KC)],
                             [wo_hi[:, c, :] for c in range(KC)], [wo_lo[:, c, :] for c in range(KC)])\
                        .then_inc(w_ps, 1)

            def value_products(base, u):
                g = group(base, u, LAG_PV)
                if g is not None:
                    pe.wait_ge(probsT_ready, g + 1)
                    pe.wait_ge(v_ready, g + 1)
                    if later(g, 1):
                        pe.wait_ge(o_ready, g)
                    for hq in range(HEADS // 4):
                        for j in range(4):
                            c, e = hq // 2, hq % 2
                            head = HC * c + 2 * j + e
                            column = HC * c + NB * e + j
                            dst = p_o[32 * j:32 * j + 32, 0:GB * HEADS // 4 * VW]\
                                .rearrange("p (b n f) -> p b n f", b=GB, f=VW)[:, :, hq, :]
                            last = pe.matmul(dst, probsT[:, (u - LAG_PV) % 2, column, :],
                                             v_diag[:, (u - LAG_PV) % 4, :, head, :], start=True, stop=True)
                    last.then_inc(o_ps, 1)

            def body(base, u):
                if filling(base, u):
                    input_transposes(base, u)
                    query_key_products(base, u)
                else:
                    query_key_products(base, u)
                    input_transposes(base, u)
                g = group(base, u, LAG_V)
                if not isinstance(base, int):
                    pe.wait_ge(v_ready, g)
                elif base + u > LAG_V:
                    pe.wait_ge(v_ready, min(base + u - LAG_V, NG))
                if not draining(base, u):
                    result_transposes(base, u)
                if g is not None:
                    hi, lo = projection_input(u, LAG_V)
                    products(p_v, hi, lo, [wqkv_hi[:, c, 2 * D:3 * D] for c in range(KC)],
                             [wqkv_lo[:, c, 2 * D:3 * D] for c in range(KC)]).then_inc(v_ps, 1)
                if draining(base, u) and FIRST_GATES[base + u - NG - LAG_QKT]:
                    pe.wait_ge(hh_loaded, 16)
                    pe.wait_ge(qkT_ready, NG)
                    pe.wait_ge(qkn_ready, NG)
                    for c, k in FIRST_GATES[base + u - NG - LAG_QKT]:
                        state_gates(0, c, k, opens=True)
                g = group(base, u, LAG_S)
                if g is not None:
                    slot = (u - LAG_S) % 2
                    pe.wait_ge(k_diag_ready[slot], spread(g, slot))
                    if later(g, 1):
                        pe.wait_ge(logits_ready, g)
                    for c in range(KC):
                        for b in range(GB):
                            last = pe.matmul(p_s[T * b:T * b + T, c * HC * T:(c + 1) * HC * T]
                                             .rearrange("p (r n k) -> p n r k", r=2, k=T),
                                             qkT[:, slot, c * P + T * b:c * P + T * b + T],
                                             k_diag[:, slot, :, :, GB * c + b, :], start=True, stop=True)
                    last.then_inc(s_ps, 1)
                g = group(base, u, LAG_QKT)
                if g is not None:
                    slot = (u - LAG_QKT) % 2
                    pe.wait_ge(qkn_ready, g + 1)
                    if later(g, 1):
                        pe.wait_ge(qkT_ready, g)
                    for m in range(2 * KC):
                        last = pe.transpose(p_qkT[:, m * P:m * P + P], qkn[:, slot, m * P:m * P + P], ident[:, :])
                    last.then_inc(qkT_ps, 1)
                value_products(base, u)
                if draining(base, u):
                    result_transposes(base, u)
                output_projection(base, u)

            pipeline(pe, body, NG - 1 + LAG_X2T)

            def output_transposes(t, s, slot):
                pe.wait_ge(yT_ready, t + 1)
                if later(t, 1):
                    pe.wait_ge(y_ready, t)
                for c in range(KC):
                    last = pe.transpose(gru_bank(slot, c, 1)[:, SPARE_COL:SPARE_COL + P], yT[:, s % 2, c, :],
                                        ident[:, :])
                last.then_inc(y_ps, 1)

            pe.wait_ge(x2T_ready, NG)
            pe.wait_ge(wih_ready, KC)
            for c in range(KC):
                first_input_gates(c).then_inc(gates_ps[c], 1)

            def step(base, s):
                t = base + s
                slot, e = s // 2, s % 2
                if later(t, 1):
                    pe.wait_ge(h_ready[0], t)
                    state_gates(s, 0, 0)
                    pe.wait_ge(h_ready[1], t)
                    state_gates(s, 0, 1).then_inc(gates_ps[0], 1)
                    output_transposes(t - 1, (s - 1) % 4, 1 - slot)
                    state_gates(s, 1, 0)
                    state_gates(s, 1, 1).then_inc(gates_ps[1], 1)
                if has_pair(base, s // 2 + 1):
                    pe.wait_ge(pair_lo_ready, pair_index(base, s // 2 + 1) + 1)
                    input_gates(1 - slot, e, 0)
                    if later(t, 1):
                        pe.wait_ge(y_ready, t)
                    input_gates(1 - slot, e, 1)

            gru_steps(pe, step)
            output_transposes(T - 1, 3, 0)


_INS = ['x', 'cond_2048', 'L0_cond_W_emb', 'L0_cond_b_emb', 'L0_cond_g_norm', 'L0_cond_W_qkv', 'L0_cond_g_q',
        'L0_cond_g_k', 'L0_cond_W_out', 'L1_cond_W_ih', 'L1_cond_W_hh', 'L1_cond_b_ih', 'L1_cond_b_hh']
_OUTS = [((B, T, D), 'float32')]


def kernel(**inputs):
    import numpy as _np
    import concourse.bacc as _bacc
    from concourse import mybir as _mybir
    from concourse.bass_utils import run_bass_kernel_spmd as _run

    nc = _bacc.Bacc("TRN2", target_bir_lowering=False, num_devices=1)
    arrays, args = {}, []
    for name in _INS:
        a = _np.ascontiguousarray(inputs[name])
        arrays[f"in_{name}_dram"] = a
        args.append(nc.dram_tensor(f"in_{name}_dram", a.shape, _mybir.dt.from_np(a.dtype), kind="ExternalInput").ap())
    for i, (shape, dtype) in enumerate(_OUTS):
        dt = _mybir.dt.from_np(_np.dtype(dtype))
        args.append(nc.dram_tensor(f"out_{i}_dram", shape, dt, kind="ExternalOutput").ap())
    adaptive_attention_gru(nc, *args)
    r = _run(nc, [arrays], core_ids=[0])
    return r.results[0]["out_0_dram"]
```
